# Optimizing a Trainium2 kernel written in Bass

```python
import numpy as np
import jax
import jax.numpy as jnp

def _softmax(x, axis=-1):
    return jax.nn.softmax(x, axis=axis)

def _gelu(x):
    return jax.nn.gelu(x, approximate=True)

def _silu(x):
    return jax.nn.silu(x)

def _sigmoid(x):
    return jax.nn.sigmoid(x)

def _layernorm(x, axis=-1, eps=1e-05):
    m = jnp.mean(x, axis=axis, keepdims=True)
    v = jnp.var(x, axis=axis, keepdims=True)
    return (x - m) / jnp.sqrt(v + eps)

def _scatter_add(tgt, idx, src, axis=0):
    return tgt.at[idx].add(src)

def _segment_sum(src, seg, n):
    return jax.ops.segment_sum(src, seg, n)
kernel_name = 'mk_xattn_ffn_d2_seqx_r4_4503e3'

def setup_inputs(seed: int=0):
    np.random.seed(seed)
    _w = jnp.asarray

    def _rec_inputs():
        import jax
        import jax.numpy as jnp
        _rk = jax.random.key(seed)
        x = 7.22e-05 + 1 * jax.random.normal(jax.random.fold_in(_rk, 1), (2, 512, 512), jnp.float32)
        _lenS = 512 - jax.random.randint(jax.random.fold_in(_rk, 7), (2,), 0, max(1, 512 // 4) + 1, jnp.int32)
        _lenS2 = 1024 - jax.random.randint(jax.random.fold_in(_rk, 8), (2,), 0, max(1, 1024 // 4) + 1, jnp.int32)
        _ctx_2048P = jax.random.normal(jax.random.fold_in(_rk, 11), (2, 16, 512), jnp.float32)
        _ctx_2048c = jax.random.dirichlet(jax.random.fold_in(_rk, 511), 0.3 * jnp.ones((16,), jnp.float32), (2, 1024))
        _ctx_2048t = jnp.einsum('bsk,bkd->bsd', _ctx_2048c, _ctx_2048P)
        _ctx_2048t = _ctx_2048t * jax.lax.rsqrt(jnp.mean(jnp.square(_ctx_2048t)) + 1e-12) * 0.953939
        ctx_2048 = 4.13588e-05 + 0.999923 * (_ctx_2048t + 0.3 * jax.random.normal(jax.random.fold_in(_rk, 611), (2, 1024, 512), jnp.float32))
        return (x, ctx_2048)
    x, ctx_2048 = _rec_inputs()

    def _L0_xattn_setup():
        import math
        import jax, jax.numpy as jnp
        import numpy as np
        HEADS = 16
        MASKED_BIAS = -10000.0

        def _mha(q, k, v):
            B, Sq, D = q.shape
            Sk = k.shape[-2]
            hd = D // HEADS
            qh = q.reshape(B, Sq, HEADS, hd).transpose(0, 2, 1, 3)
            kh = k.reshape(B, Sk, HEADS, hd).transpose(0, 2, 1, 3)
            vh = v.reshape(B, Sk, HEADS, hd).transpose(0, 2, 1, 3)
            scores = jnp.einsum('bhqd,bhkd->bhqk', qh, kh) / math.sqrt(hd)
            qi = jnp.arange(Sq)[:, None] + (Sk - Sq)
            ki = jnp.arange(Sk)[None, :]
            causal = ki <= qi
            scores = jnp.where(causal[None, None], scores, jnp.asarray(MASKED_BIAS, scores.dtype))
            attn = jax.nn.softmax(scores, axis=-1)
            out = jnp.einsum('bhqk,bhkd->bhqd', attn, vh)
            return out.transpose(0, 2, 1, 3).reshape(B, Sq, D)
        key = jax.random.key(seed)
        kq, kk, kv = jax.random.split(key, 3)
        B, S, D = (4, 256, 512)
        q = jax.random.normal(kq, (B, S, D), dtype=jnp.float32)
        k = jax.random.normal(kk, (B, S, D), dtype=jnp.float32)
        v = jax.random.normal(kv, (B, S, D), dtype=jnp.float32)
        return {'q': q, 'k': k, 'v': v}
    _L0_xattn_all = _L0_xattn_setup()
    _L0_xattn_in = {k: v for k, v in _L0_xattn_all.items() if k in ()}
    del _L0_xattn_all

    def _L0_ffn_setup():
        import jax, jax.numpy as jnp
        import numpy as np
        NUM_EXPERTS = 8
        TOP_K = 2
        FFN_DIM = 512
        HIDDEN_DIM = 1024
        key = jax.random.key(seed)
        k0, k1, k2, k3, k4 = jax.random.split(key, 5)
        scale = 0.02
        return {'hidden_states': jax.random.normal(k0, (2, 256, FFN_DIM), dtype=jnp.float32), 'gate_w': jax.random.normal(k1, (NUM_EXPERTS, FFN_DIM), dtype=jnp.float32) * scale, 'w1': jax.random.normal(k2, (NUM_EXPERTS, FFN_DIM, HIDDEN_DIM), dtype=jnp.float32) * scale, 'w2': jax.random.normal(k3, (NUM_EXPERTS, HIDDEN_DIM, FFN_DIM), dtype=jnp.float32) * scale, 'w3': jax.random.normal(k4, (NUM_EXPERTS, FFN_DIM, HIDDEN_DIM), dtype=jnp.float32) * scale}
    _L0_ffn_all = _L0_ffn_setup()
    _L0_ffn_in = {k: v for k, v in _L0_ffn_all.items() if k in ('gate_w', 'w1', 'w2', 'w3')}
    del _L0_ffn_all

    def _L1_xattn_setup():
        import jax, jax.numpy as jnp
        import numpy as np
        D_MODEL = 512
        NUM_HEADS = 16
        HEAD_DIM = D_MODEL // NUM_HEADS

        def _fq_sym(x, axis):
            s = jnp.max(jnp.abs(x), axis=axis, keepdims=True) / 127.0
            s = jnp.maximum(s, 1e-08)
            q = jnp.clip(jnp.round(x / s), -127.0, 127.0) * s
            return x + jax.lax.stop_gradient(q - x)

        def _fq_unsigned(x, axis):
            s = jnp.max(x, axis=axis, keepdims=True) / 255.0
            s = jnp.maximum(s, 1e-08)
            q = jnp.clip(jnp.round(x / s), 0.0, 255.0) * s
            return x + jax.lax.stop_gradient(q - x)
        key = jax.random.key(seed)
        ks = jax.random.split(key, 8)
        B, N, M, C = (2, 512, 128, D_MODEL)
        return {'x': jax.random.normal(ks[0], (B, N, C), jnp.float32), 'cond': jax.random.normal(ks[1], (B, M, C), jnp.float32), 'Wq': jax.random.normal(ks[2], (C, C), jnp.float32) * 0.02, 'bq': jnp.zeros((C,), jnp.float32), 'Wkv': jax.random.normal(ks[3], (C, 2 * C), jnp.float32) * 0.02, 'bkv': jnp.zeros((2 * C,), jnp.float32), 'Wp': jax.random.normal(ks[4], (C, C), jnp.float32) * 0.02, 'bp': jnp.zeros((C,), jnp.float32)}
    _L1_xattn_all = _L1_xattn_setup()
    _L1_xattn_in = {k: v for k, v in _L1_xattn_all.items() if k in ('Wq', 'bq', 'Wkv', 'bkv', 'Wp', 'bp')}
    del _L1_xattn_all

    def _L1_ffn_setup():
        import jax, jax.numpy as jnp
        import numpy as np
        EPS = 1e-05
        RMS_EPS = 1e-06

        def activation_quant(x, num_bits=8):
            qn = -2 ** (num_bits - 1)
            qp = 2 ** (num_bits - 1) - 1
            xf = x.astype(jnp.float32)
            s = qp / jnp.clip(jnp.max(jnp.abs(xf), axis=-1, keepdims=True), EPS, None)
            return (jnp.clip(jnp.round(xf * s), qn, qp) / s).astype(x.dtype)

        def weight_quant(w):
            wf = w.astype(jnp.float32)
            s = 1.0 / jnp.clip(jnp.mean(jnp.abs(wf)), EPS, None)
            return (jnp.clip(jnp.round(wf * s), -1.0, 1.0) / s).astype(w.dtype)

        def bit_linear(x, w):
            qx = x + jax.lax.stop_gradient(activation_quant(x) - x)
            qw = w + jax.lax.stop_gradient(weight_quant(w) - w)
            return jnp.einsum('bsh,oh->bso', qx, qw)

        def rms_norm(x, weight, eps=RMS_EPS):
            xf = x.astype(jnp.float32)
            var = jnp.mean(xf * xf, axis=-1, keepdims=True)
            return weight * (xf * jax.lax.rsqrt(var + eps)).astype(x.dtype)
        key = jax.random.key(seed)
        k1, k2, k3, k4 = jax.random.split(key, 4)
        B, S, H, I = (2, 512, 512, 2048)
        scale = 1.0 / np.sqrt(H)
        return {'x': jax.random.normal(k1, (B, S, H), dtype=jnp.float32), 'w_gate': jax.random.normal(k2, (I, H), dtype=jnp.float32) * scale, 'w_up': jax.random.normal(k3, (I, H), dtype=jnp.float32) * scale, 'w_down': jax.random.normal(k4, (H, I), dtype=jnp.float32) * (1.0 / np.sqrt(I)), 'ln_weight': jnp.ones((I,), dtype=jnp.float32)}
    _L1_ffn_all = _L1_ffn_setup()
    _L1_ffn_in = {k: v for k, v in _L1_ffn_all.items() if k in ('w_gate', 'w_up', 'w_down', 'ln_weight')}
    del _L1_ffn_all
    return {'x': x, 'ctx_2048': ctx_2048, 'L0_ffn_gate_w': _L0_ffn_in['gate_w'], 'L0_ffn_w1': _L0_ffn_in['w1'], 'L0_ffn_w2': _L0_ffn_in['w2'], 'L0_ffn_w3': _L0_ffn_in['w3'], 'L1_xattn_Wq': _L1_xattn_in['Wq'], 'L1_xattn_bq': _L1_xattn_in['bq'], 'L1_xattn_Wkv': _L1_xattn_in['Wkv'], 'L1_xattn_bkv': _L1_xattn_in['bkv'], 'L1_xattn_Wp': _L1_xattn_in['Wp'], 'L1_xattn_bp': _L1_xattn_in['bp'], 'L1_ffn_w_gate': _L1_ffn_in['w_gate'], 'L1_ffn_w_up': _L1_ffn_in['w_up'], 'L1_ffn_w_down': _L1_ffn_in['w_down'], 'L1_ffn_ln_weight': _L1_ffn_in['ln_weight']}

def reference(x, ctx_2048, L0_ffn_gate_w, L0_ffn_w1, L0_ffn_w2, L0_ffn_w3, L1_xattn_Wq, L1_xattn_bq, L1_xattn_Wkv, L1_xattn_bkv, L1_xattn_Wp, L1_xattn_bp, L1_ffn_w_gate, L1_ffn_w_up, L1_ffn_w_down, L1_ffn_ln_weight):
    import jax
    import jax.numpy as jnp

    def _L0_xattn_ref(q, k, v):
        import math
        import jax, jax.numpy as jnp
        import numpy as np
        HEADS = 16
        MASKED_BIAS = -10000.0

        def _mha(q, k, v):
            B, Sq, D = q.shape
            Sk = k.shape[-2]
            hd = D // HEADS
            qh = q.reshape(B, Sq, HEADS, hd).transpose(0, 2, 1, 3)
            kh = k.reshape(B, Sk, HEADS, hd).transpose(0, 2, 1, 3)
            vh = v.reshape(B, Sk, HEADS, hd).transpose(0, 2, 1, 3)
            scores = jnp.einsum('bhqd,bhkd->bhqk', qh, kh) / math.sqrt(hd)
            qi = jnp.arange(Sq)[:, None] + (Sk - Sq)
            ki = jnp.arange(Sk)[None, :]
            causal = ki <= qi
            scores = jnp.where(causal[None, None], scores, jnp.asarray(MASKED_BIAS, scores.dtype))
            attn = jax.nn.softmax(scores, axis=-1)
            out = jnp.einsum('bhqk,bhkd->bhqd', attn, vh)
            return out.transpose(0, 2, 1, 3).reshape(B, Sq, D)
        return _mha(q, k, v)

    def _L0_ffn_ref(hidden_states, gate_w, w1, w2, w3):
        import jax, jax.numpy as jnp
        import numpy as np
        NUM_EXPERTS = 8
        TOP_K = 2
        FFN_DIM = 512
        HIDDEN_DIM = 1024
        origin_shape = hidden_states.shape
        x = hidden_states.reshape(-1, FFN_DIM)
        n_tokens = x.shape[0]
        router_logits = x @ gate_w.T
        routing_probs = jax.nn.softmax(router_logits.astype(jnp.float32), axis=-1)
        topk_w, topk_idx = jax.lax.top_k(routing_probs, TOP_K)
        topk_w = topk_w / jnp.sum(topk_w, axis=-1, keepdims=True)
        topk_w = topk_w.astype(x.dtype)
        token_ids = jnp.arange(n_tokens)[:, None]
        full_w = jnp.zeros((n_tokens, NUM_EXPERTS), dtype=x.dtype)
        full_w = full_w.at[token_ids, topk_idx].add(topk_w)
        h = jax.nn.silu(jnp.einsum('nf,efh->enh', x, w1)) * jnp.einsum('nf,efh->enh', x, w3)
        y = jnp.einsum('enh,ehf->enf', h, w2)
        out = jnp.einsum('enf,ne->nf', y, full_w)
        return out.reshape(origin_shape)

    def _L1_xattn_ref(x, cond, Wq, bq, Wkv, bkv, Wp, bp):
        import jax, jax.numpy as jnp
        import numpy as np
        D_MODEL = 512
        NUM_HEADS = 16
        HEAD_DIM = D_MODEL // NUM_HEADS

        def _fq_sym(x, axis):
            s = jnp.max(jnp.abs(x), axis=axis, keepdims=True) / 127.0
            s = jnp.maximum(s, 1e-08)
            q = jnp.clip(jnp.round(x / s), -127.0, 127.0) * s
            return x + jax.lax.stop_gradient(q - x)

        def _fq_unsigned(x, axis):
            s = jnp.max(x, axis=axis, keepdims=True) / 255.0
            s = jnp.maximum(s, 1e-08)
            q = jnp.clip(jnp.round(x / s), 0.0, 255.0) * s
            return x + jax.lax.stop_gradient(q - x)
        B, N, C = x.shape
        H, hd = (NUM_HEADS, HEAD_DIM)
        q = (x @ Wq + bq).reshape(1, B * N, H, hd)
        kv = (cond @ Wkv + bkv).reshape(1, -1, 2, H, hd)
        k, v = (kv[:, :, 0], kv[:, :, 1])
        scale = 1.0 / np.sqrt(hd).astype(np.float32)
        q = jnp.transpose(q * scale, (0, 2, 1, 3))
        k = jnp.transpose(k, (0, 2, 1, 3))
        v = jnp.transpose(v, (0, 2, 1, 3))
        q = _fq_sym(q, axis=-1)
        k = _fq_sym(k, axis=-1)
        v = _fq_sym(v, axis=2)
        attn = jnp.einsum('bhqd,bhkd->bhqk', q, k)
        attn = jax.nn.softmax(attn.astype(jnp.float32), axis=-1)
        attn = _fq_unsigned(attn, axis=-1)
        out = jnp.einsum('bhqk,bhkd->bhqd', attn, v)
        out = jnp.transpose(out, (0, 2, 1, 3)).reshape(B, N, C)
        return out @ Wp + bp

    def _L1_ffn_ref(x, w_gate, w_up, w_down, ln_weight):
        import jax, jax.numpy as jnp
        import numpy as np
        EPS = 1e-05
        RMS_EPS = 1e-06

        def activation_quant(x, num_bits=8):
            qn = -2 ** (num_bits - 1)
            qp = 2 ** (num_bits - 1) - 1
            xf = x.astype(jnp.float32)
            s = qp / jnp.clip(jnp.max(jnp.abs(xf), axis=-1, keepdims=True), EPS, None)
            return (jnp.clip(jnp.round(xf * s), qn, qp) / s).astype(x.dtype)

        def weight_quant(w):
            wf = w.astype(jnp.float32)
            s = 1.0 / jnp.clip(jnp.mean(jnp.abs(wf)), EPS, None)
            return (jnp.clip(jnp.round(wf * s), -1.0, 1.0) / s).astype(w.dtype)

        def bit_linear(x, w):
            qx = x + jax.lax.stop_gradient(activation_quant(x) - x)
            qw = w + jax.lax.stop_gradient(weight_quant(w) - w)
            return jnp.einsum('bsh,oh->bso', qx, qw)

        def rms_norm(x, weight, eps=RMS_EPS):
            xf = x.astype(jnp.float32)
            var = jnp.mean(xf * xf, axis=-1, keepdims=True)
            return weight * (xf * jax.lax.rsqrt(var + eps)).astype(x.dtype)
        h = jax.nn.silu(bit_linear(x, w_gate)) * bit_linear(x, w_up)
        h = rms_norm(h, ln_weight)
        return bit_linear(h, w_down)
    x = x + _L0_xattn_ref(_layernorm(x, axis=-1), ctx_2048, ctx_2048)
    x = x + _L0_ffn_ref(_layernorm(x, axis=-1), L0_ffn_gate_w, L0_ffn_w1, L0_ffn_w2, L0_ffn_w3)
    x = x + _L1_xattn_ref(_layernorm(x, axis=-1), ctx_2048, L1_xattn_Wq, L1_xattn_bq, L1_xattn_Wkv, L1_xattn_bkv, L1_xattn_Wp, L1_xattn_bp)
    x = x + _L1_ffn_ref(_layernorm(x, axis=-1), L1_ffn_w_gate, L1_ffn_w_up, L1_ffn_w_down, L1_ffn_ln_weight)
    return x

_drawn_inputs = setup_inputs


def setup_inputs(seed=0):
    import zlib

    import numpy as np

    out = dict(_drawn_inputs(seed))
    spreads = {'L1_xattn_bq': (0.0, 2.0),
     'L1_xattn_bkv': (0.0, 0.1),
     'L1_xattn_bp': (0.0, 0.1),
     'L1_ffn_ln_weight': (1.0, 0.2)}
    factors = {'L1_xattn_Wq': 3.867}
    for name, (base, spread) in spreads.items():
        noise = np.random.default_rng([zlib.crc32(name.encode()), seed]).standard_normal(out[name].shape)
        drawn = base * np.exp(spread * noise) if base else spread * noise
        out[name] = jnp.asarray(drawn.astype(out[name].dtype))
    for name, factor in factors.items():
        out[name] = (out[name] * factor).astype(out[name].dtype)
    return out
```

```python
from contextlib import ExitStack

import concourse.bass as bass
from concourse import mybir

F32 = mybir.dt.float32
BF16 = mybir.dt.bfloat16
F16 = mybir.dt.float16
I16 = mybir.dt.int16
I32 = mybir.dt.int32
U8 = mybir.dt.uint8
ALU = mybir.AluOpType
ACT = mybir.ActivationFunctionType
X = mybir.AxisListType.X
BYTES = {F32: 4, I32: 4, BF16: 2, F16: 2, I16: 2, U8: 1}

P = 128
B, SQ, SK, D = 2, 512, 1024, 512
H, HD = 16, 32
T = B * SQ
NT = T // P
NC = B * SK // P
KC = D // P
E, EH = 8, 1024
EC = EH // P
SLOTS = 2 * T // P + E - 1
FI = 2048
FC = FI // P
UNITS = B * H
QT, KT = SQ // P, SK // P
HALF = KT - QT
WID = [SQ if k < HALF else SQ - P * (k - HALF) for k in range(KT)]
OFF = [sum(WID[:k]) for k in range(KT)]
NP = sum(WID)
KBLK, QBLK = 4, 5
KROW = KBLK * HD + 2
QROW = QBLK * HD
K3 = 3 * HD
MAGIC = 12582912.0
LN255 = 5.541263545158426
MASKED = -1.0e30
SCALE = float(HD) ** -0.5
LN_EPS, RMS_EPS = 1e-5, 1e-6
CONSTS = 13
V_STEPS = 5
LN_STEPS = 3 * NT + 6
R_ASSIGNED, R_STEPS = 17, 36
F_STEPS_Q = 7 + 2 * NT
FW_GROUPS = 2 * FC + 2 * KC


def at(u):
    return u + 1


def sweep(eng, n, body):
    body(0, 0, 0, True, n == 1)
    pairs = (n - 2) // 2
    if pairs > 0:
        with eng.Fori(0, pairs) as i:
            body(2 * i + 1, 1, i, False, False)
            body(2 * i + 2, 0, i + 1, False, False)
    for u in range(1 + 2 * max(pairs, 0), n):
        body(u, u % 2, u // 2, False, u == n - 1)


def turn_rows(pe, rows, ready, base, turned, copied, banks, ident):
    for t in range(NT):
        pe.wait_ge(ready, base + t + 1)
        if t >= 2:
            pe.wait_ge(copied, t - 1)
        for c in range(KC):
            ins = pe.transpose(banks[t % 2][:, c * P:(c + 1) * P], rows[:, t, c * P:(c + 1) * P], ident)
        ins.then_inc(turned, 1)


def program(nc, x, ctx_in, gate_w, w1, w2, w3, Wq, bq, Wkv, bkv, Wp, bp, w_gate, w_up, w_down, ln_w, out):
    with ExitStack() as stack:
        def sem(name):
            return stack.enter_context(nc.semaphore(name))

        ARENA = 207 * 1024
        arena = stack.enter_context(nc.sbuf_tensor("arena", [P, ARENA], U8))
        scores = stack.enter_context(nc.psum_tensor("scores", [P, 4 * 512], F32))
        bank4 = stack.enter_context(nc.psum_tensor("bank4", [P, 512], F32))
        bank5 = stack.enter_context(nc.psum_tensor("bank5", [P, 512], F32))
        bank6 = stack.enter_context(nc.psum_tensor("bank6", [P, 512], F32))
        bank7 = stack.enter_context(nc.psum_tensor("bank7", [P, 512], F32))

        class Region:

            def __init__(self, start, end=ARENA):
                self.at, self.end = start, end

            def take(self, dtype, *shape):
                n = BYTES[dtype]
                for s in shape:
                    n *= s
                view = arena[:, self.at:self.at + n].bitcast(dtype)
                self.at += (n + 31) // 32 * 32
                assert self.at <= self.end, "the region is full"
                names = "abcdef"[:len(shape)]
                if len(shape) > 1:
                    sizes = {names[i]: shape[i] for i in range(len(shape))}
                    view = view.rearrange(f"p ({' '.join(names)}) -> p {' '.join(names)}", **sizes)
                return view

        kst_d = nc.dram_tensor("kst_d", (H, K3, B * SK), BF16, kind="Internal").ap()
        qst_d = nc.dram_tensor("qst_d", (H, K3, T), BF16, kind="Internal").ap()
        xs_d = nc.dram_tensor("xs_d", (SLOTS * P, D), F32, kind="Internal").ap()
        ys_d = nc.dram_tensor("ys_d", (SLOTS * P, D), F32, kind="Internal").ap()

        keep = Region(0)
        xres = keep.take(F32, NT, D)
        vint = keep.take(BF16, NC, D)
        svrow = keep.take(F32, D)
        idf = keep.take(F32, P)
        idb = keep.take(BF16, P)
        mask_q = keep.take(BF16, P)
        mask_k = keep.take(BF16, P)
        tri = keep.take(BF16, P)
        ones = keep.take(BF16, P)
        iota_e = keep.take(F32, E)
        iota_s = keep.take(F32, SLOTS + 1)
        stats = keep.take(F32, NT, 6)
        mv = keep.take(F32, NT, 2)
        std0 = keep.take(F32, NT)
        ln_t = keep.take(F32, 6, NT)
        small = keep.take(F32, 64)
        base = keep.at

        consts_made = sem("consts_made")
        x_loaded = [sem(f"x_loaded{b}") for b in range(B)]

        wkv_loaded = sem("wkv_loaded")
        ctx_loaded = [sem(f"ctx_loaded{a}") for a in range(2)]
        ctx_turned, ctxT_ready = sem("ctx_turned"), sem("ctxT_ready")
        c1_done, cr_done, c2_done, c3_done = (sem(n) for n in ("c1_done", "cr_done", "c2_done", "c3_done"))
        k_proj, v_proj, kf_done, vf_done = (sem(n) for n in ("k_proj", "v_proj", "kf_done", "vf_done"))
        kam_done, ks_done, kinv_done, kx_done, kr_done, kd_done = (
            sem(n) for n in ("kam_done", "ks_done", "kinv_done", "kx_done", "kr_done", "kd_done"))
        kq1_done, kqr_done, kq2_done, krow_ready = (sem(n) for n in ("kq1_done", "kqr_done", "kq2_done", "krow_ready"))
        k_turned, kT_ready = sem("k_turned"), sem("kT_ready")
        kst_stored = [sem(f"kst_stored{a}") for a in range(2)]
        ones_set = sem("ones_set")
        v_step, vmax_ready = sem("v_step"), sem("vmax_ready")

        rk = Region(base)
        kvrow = rk.take(BF16, B, H, KT, KROW)
        after_kvrow = rk.at
        wkv = rk.take(F32, KC, 2 * D)
        bkv_row = rk.take(F32, 2 * D)
        cin = [rk.take(F32, D) for _ in range(2)]
        cT = [rk.take(F32, KC, P) for _ in range(2)]
        cr = rk.take(F32, D)
        kf, kx, kr, kd, kqr = (rk.take(F32, H, HD) for _ in range(5))
        kam, ks, kinv = (rk.take(F32, H) for _ in range(3))
        krow = [rk.take(BF16, H, 3, HD) for _ in range(2)]
        kTbuf = [rk.take(BF16, H, P) for _ in range(2)]
        vf = rk.take(F32, NC, D)
        vam = kf.rearrange("p a b -> p (a b)")

        ra = Region(after_kvrow)
        qrow = ra.take(BF16, B, H, QT, QROW)
        kst = [ra.take(BF16, KT, KROW) for _ in range(2)]
        qst = [ra.take(BF16, QT, QROW) for _ in range(2)]
        kA = [ra.take(BF16, SK) for _ in range(2)]
        kB = [ra.take(BF16, SK) for _ in range(2)]
        qAB = [ra.take(BF16, 2, SQ) for _ in range(2)]
        oatt = ra.take(F32, B, H, QT, HD)
        xn0 = oatt.rearrange("p b h t d -> p (b h t d)").rearrange("p (t d) -> p t d", t=NT)
        qr = Region(ra.at).take(F32, NT, D)
        eP = ra.take(F32, NP)
        p1 = ra.take(F16, NP)
        p2 = ra.take(F16, NP)
        mx = ra.take(F32, QT)
        mr = ra.take(F32, QT)
        mparts = ra.take(BF16, QT, 4)
        osum = ra.take(F32, QT, HD)
        rl = ra.take(F32, QT)

        rm = Region(base)
        wbuf = [(rm.take(F32, 2, KC, EH), rm.take(F32, EC, D)) for _ in range(2)]
        xsin = [rm.take(F32, D) for _ in range(2)]
        xsT = [rm.take(F32, KC, P) for _ in range(2)]
        sg = rm.take(F32, EH)
        hb = rm.take(F32, EH)
        hT = rm.take(F32, EC, P)
        yb = [rm.take(F32, D) for _ in range(2)]
        xn = rm.take(F32, NT, D)
        XT = rm.take(F32, KC, T)
        gw = rm.take(F32, D)
        gwT = rm.take(F32, KC, E)
        zero = rm.take(F32, D)
        r8 = [rm.take(F32, NT, E) for _ in range(12)]
        r1 = [rm.take(F32, NT) for _ in range(10)]
        asg = rm.take(BF16, NT, E)
        te = [rm.take(F32, E) for _ in range(6)]
        posi = rm.take(I32, 2, NT)
        cmp = rm.take(F32, SLOTS + 1, E)
        slot_f = rm.take(F32, SLOTS + 1)
        slot_e = rm.take(I32, SLOTS + 1)
        gath = Region(base)
        grow = [gath.take(F32, D) for _ in range(2 * NT)]

        rq = Region(base)
        xn3 = rq.take(F32, NT, D)
        XT3 = rq.take(F32, KC, T)
        wq_sb = rq.take(F32, KC, D)
        bq_row = rq.take(F32, D)
        wp_sb = rq.take(F32, KC, D)
        bp_row = rq.take(F32, D)
        qf, qx = (rq.take(F32, H, HD) for _ in range(2))
        qam, qsv, qinv = (rq.take(F32, H) for _ in range(3))
        nsq = rq.take(F32, H, NT)
        q3row = [rq.take(BF16, H, 3, HD) for _ in range(2)]
        qTbuf = [rq.take(BF16, H, P) for _ in range(2)]
        khead = [rq.take(BF16, B * SK) for _ in range(2)]
        qhead = [rq.take(BF16, T) for _ in range(2)]
        vhead = [rq.take(BF16, NC, HD) for _ in range(2)]
        ssb = [rq.take(F32, B * SK) for _ in range(2)]
        nmx = [rq.take(F32, 2) for _ in range(2)]
        ebias = [rq.take(F32, 1) for _ in range(2)]
        p16 = [rq.take(I16, B * SK) for _ in range(2)]
        pT = [rq.take(BF16, NC, P) for _ in range(2)]
        rsum = [rq.take(F32, NT) for _ in range(2)]
        rrec = rq.take(F32, NT)
        otmp = rq.take(F32, NT, HD)
        oh = rq.take(F32, NT, D)

        rf = Region(base)
        xn4 = rf.take(F32, NT, D)
        xq4 = rf.take(BF16, NT, D)
        xT4 = rf.take(BF16, KC, T)
        wT = [rf.take(BF16, KC, FI) for _ in range(2)]
        wdT = rf.take(BF16, FC, D)
        lnw = rf.take(F32, FI)
        am4, sx4, sr4 = (rf.take(F32, NT) for _ in range(3))
        wsum = rf.take(F32, FC)
        wst = rf.take(F32, 12)
        gscale = rf.take(F32, 2, NT)
        ssq = rf.take(F32, NT)
        fsm = rf.take(F32, 12, NT)
        f_mark = rf.at
        wld = rf.take(F32, FC, D)
        wtmp = rf.take(F32, 2, FC // 2, D)
        wint = rf.take(BF16, FC, D)
        rg = Region(f_mark)
        hball = rg.take(F32, NT, FI)
        sgb = rg.take(F32, FI)
        hqr = rg.take(BF16, FI)
        hqT = rg.take(BF16, FC, P)

        def context_parts(u):
            rows = kvrow.rearrange("p b h t c -> p b h (t c)")
            view = rows[:, bass.ds(u // KT, 1), :, bass.ds((u % KT) * KROW, KBLK * HD)]
            return view.rearrange("p b h (c d) -> p (b h) c d", d=HD)

        def by_head(row):
            return row.rearrange("p (h d) -> p h d", h=H)

        def each(col, shape):
            return col.rearrange("p (n o) -> p n o", o=1).broadcast_to([P] + shape)

        x_t = x.rearrange("b (t p) d -> p (b t) d", p=P)
        out_t = out.rearrange("b (t p) d -> p (b t) d", p=P)
        ctx_t = ctx_in.rearrange("b (t p) d -> (b t) p d", p=P)

        ln_step, ln_var, ln_std = sem("ln_step"), sem("ln_var"), sem("ln_std")
        qs1, qs_r, qs2, qs3 = (sem(n) for n in ("qs1", "qs_r", "qs2", "qs3"))
        staged = sem("staged")
        ka_turned, kb_turned, q_turned, m_turned = (sem(n) for n in ("ka_turned", "kb_turned", "q_turned", "m_turned"))
        ka_ready, kb_ready, qab_ready, m_ready = (sem(n) for n in ("ka_ready", "kb_ready", "qab_ready", "m_ready"))
        smax_done, max_done, m_step = sem("smax_done"), sem("max_done"), sem("m_step")
        st_done, exp_done, p1_done, p2_done = (sem(n) for n in ("st_done", "exp_done", "p1_done", "p2_done"))
        pv_done, osum_done, rl_done, o_done = (sem(n) for n in ("pv_done", "osum_done", "rl_done", "o_done"))
        att_added = sem("att_added")
        gw_loaded, xs_zeroed = sem("gw_loaded"), sem("xs_zeroed")
        zero_made = sem("zero_made")
        gw_turned, gwT_ready = sem("gw_turned"), sem("gwT_ready")
        xn_turned, xT_ready, logits_done = sem("xn_turned"), sem("xT_ready"), sem("logits_done")
        r_step, r_exp, ranks_done = sem("r_step"), sem("r_exp"), sem("ranks_done")
        scattered = sem("scattered")
        gathered = [sem(f"gathered{t}") for t in range(NT)]
        w_loaded = [sem(f"w_loaded{a}") for a in range(2)]
        xs_loaded = [sem(f"xs_loaded{a}") for a in range(2)]
        xs_turned, xsT_ready = sem("xs_turned"), sem("xsT_ready")
        up_done, silu_done, h_done = sem("up_done"), sem("silu_done"), sem("h_done")
        h_turned, hT0_ready, hT1_ready = sem("h_turned"), sem("hT0_ready"), sem("hT1_ready")
        y_done, y_ready = sem("y_done"), sem("y_ready")
        y_stored = [sem(f"y_stored{a}") for a in range(2)]
        moe_added = sem("moe_added")
        wq_loaded, wp_loaded = sem("wq_loaded"), sem("wp_loaded")
        x3_turned, x3T_ready = sem("x3_turned"), sem("x3T_ready")
        q_proj, qf_done, q_step, q3_ready = (sem(n) for n in ("q_proj", "qf_done", "q_step", "q3_ready"))
        q3_turned, qT_ready = sem("q3_turned"), sem("qT_ready")
        qst_stored = [sem(f"qst_stored{a}") for a in range(2)]
        k_loaded = [sem(f"k_loaded{a}") for a in range(2)]
        v_staged = sem("v_staged")
        s_done, s_read, bias_ready = sem("s_done"), sem("s_read"), sem("bias_ready")
        p_ready, p_turned, pT_lo, pT_hi = (sem(n) for n in ("p_ready", "p_turned", "pT_lo", "pT_hi"))
        av_done, a_post = sem("av_done"), sem("a_post")
        o_turned, oT_ready, o_proj, o_added = (sem(n) for n in ("o_turned", "oT_ready", "o_proj", "o_added"))
        fw_loaded, lnw_loaded = sem("fw_loaded"), sem("lnw_loaded")
        fw_step, fw_sum, fw_all, fw_int = (sem(n) for n in ("fw_step", "fw_sum", "fw_all", "fw_int"))
        fw_turned, fwT_ready = sem("fw_turned"), sem("fwT_ready")
        f_step, x4_turned, x4T_ready = sem("f_step"), sem("x4_turned"), sem("x4T_ready")
        gu_done, fsilu_done, fh_done, fsq_done, fy_done = (
            sem(n) for n in ("gu_done", "fsilu_done", "fh_done", "fsq_done", "fy_done"))
        f2_step, fh_turned, fhT_ready, fdown_done, fout_done = (
            sem(n) for n in ("f2_step", "fh_turned", "fhT_ready", "fdown_done", "fout_done"))
        f_var, f_std = sem("f_var"), sem("f_std")
        stored = sem("stored")

        block = stack.enter_context(nc.Block())

        @block.sync
        def _(sp):
            sp.dma_start(wkv, Wkv.rearrange("(k p) n -> p k n", p=P)).then_inc(wkv_loaded, 16)
            sp.dma_start(bkv_row, bkv.partition_broadcast(P)).then_inc(wkv_loaded, 16)

            def load_ctx(u, a, k, first, last):
                if not first:
                    sp.wait_ge(ctx_turned, at(u - 2))
                    sp.wait_ge(c1_done, at(u - 2))
                    sp.wait_ge(cr_done, at(u - 2))
                sp.dma_start(cin[a], ctx_t[bass.ds(u, 1)].rearrange("a p d -> p (a d)")).then_inc(ctx_loaded[a], 16)

            sweep(sp, NC, load_ctx)
            for b in range(B):
                sp.dma_start(xres[:, b * QT:(b + 1) * QT, :], x_t[:, b * QT:(b + 1) * QT, :]).then_inc(x_loaded[b], 16)

            sp.wait_ge(zero_made, 1)
            sp.dma_start(gw[0:E, :], gate_w).then_inc(gw_loaded, 16)
            for s in range(SLOTS):
                sp.dma_start(xs_d[s * P:(s + 1) * P, :], zero).then_inc(xs_zeroed, 16)

            sp.wait_ge(r_step, R_STEPS)
            with sp.register("expert") as expert:
                def load_slot(u, a, k, first, last):
                    sp.reg_load(expert, slot_e[0:1, bass.ds(u, 1)])
                    e = sp.snap(expert)
                    if first:
                        sp.wait_ge(scattered, 16 * 2 * NT)
                    else:
                        sp.wait_ge(xs_turned, at(u - 2))
                    sp.dma_start(xsin[a], xs_d[bass.ds(u * P, P), :]).then_inc(xs_loaded[a], 16)
                    if not first:
                        sp.wait_ge(y_done, at(u - 2))
                    sp.dma_start(wbuf[a][0][:, 0], w1[bass.ds(e, 1)].rearrange("e (k p) n -> p (e k) n", p=P)).then_inc(w_loaded[a], 16)
                    sp.dma_start(wbuf[a][0][:, 1], w3[bass.ds(e, 1)].rearrange("e (k p) n -> p (e k) n", p=P)).then_inc(w_loaded[a], 16)
                    sp.dma_start(wbuf[a][1], w2[bass.ds(e, 1)].rearrange("e (k p) n -> p (e k) n", p=P)).then_inc(w_loaded[a], 16)

                sweep(sp, SLOTS, load_slot)

            sp.wait_ge(moe_added, 2 * NT)
            sp.dma_start(wq_sb, Wq.rearrange("(k p) n -> p k n", p=P)).then_inc(wq_loaded, 16)
            sp.dma_start(bq_row, bq.partition_broadcast(P)).then_inc(wq_loaded, 16)
            sp.dma_start(wp_sb, Wp.rearrange("(k p) n -> p k n", p=P)).then_inc(wp_loaded, 16)
            sp.dma_start(bp_row, bp.partition_broadcast(P)).then_inc(wp_loaded, 16)

            for a in range(2):
                sp.wait_ge(qst_stored[a], 16 * (NT // 2))
                sp.wait_ge(kst_stored[a], 16 * (NC // 2))

            def load_head(u, a, k, first, last):
                if not first:
                    sp.wait_ge(s_done, 16 * (u - 1))
                sp.dma_start(khead[a][0:K3, :], kst_d[bass.ds(u, 1)].rearrange("h r n -> r (h n)")).then_inc(k_loaded[a], 16)
                sp.dma_start(qhead[a][0:K3, :], qst_d[bass.ds(u, 1)].rearrange("h r n -> r (h n)")).then_inc(k_loaded[a], 16)

            sweep(sp, H, load_head)

            sp.wait_ge(o_added, 2 * NT)
            sp.dma_start(lnw, ln_w.partition_broadcast(P)).then_inc(lnw_loaded, 16)
            for w, src in enumerate((w_gate, w_up)):
                if w:
                    sp.wait_ge(fw_int, 2 * w)
                sp.dma_start(wld, src.rearrange("(o p) n -> p o n", p=P)).then_inc(fw_loaded, 16)
            sp.wait_ge(fw_int, 4)
            sp.dma_start(wld.rearrange("p (o c) n -> p o (c n)", o=KC), w_down.rearrange("(o p) n -> p o n", p=P)).then_inc(fw_loaded, 16)

            for t in range(NT):
                sp.wait_ge(fout_done, at(t))
                sp.dma_start(out_t[:, t, :], xres[:, t, :]).then_inc(stored, 16)
            sp.wait_ge(stored, 16 * NT)

        @block.gpsimd
        def _(pool):
            n = 0

            def made(ins):
                nonlocal n
                ins.then_inc(consts_made, 1)
                n += 1
                pool.wait_ge(consts_made, n)

            for m, fill in ((idf, 0.0), (idb, 0.0), (mask_q, 0.0), (mask_k, 0.0), (tri, 1.0), (ones, 1.0)):
                made(pool.memset(m, fill))
            for m in (idf, idb):
                made(pool.affine_select(out=m, in_=m, compare_op=ALU.not_equal, fill=1.0, base=0,
                                        pattern=[[-1, P]], channel_multiplier=1))
            made(pool.affine_select(out=mask_q, in_=mask_q, compare_op=ALU.is_ge, fill=MASKED, base=0,
                                    pattern=[[-1, P]], channel_multiplier=1))
            made(pool.affine_select(out=mask_k, in_=mask_k, compare_op=ALU.is_ge, fill=MASKED, base=0,
                                    pattern=[[1, P]], channel_multiplier=-1))
            made(pool.affine_select(out=tri, in_=tri, compare_op=ALU.is_gt, fill=0.0, base=0,
                                    pattern=[[1, P]], channel_multiplier=-1))
            made(pool.iota(iota_e, pattern=[[1, E]], base=0, channel_multiplier=0, allow_small_or_imprecise_dtypes=True))
            made(pool.iota(iota_s, pattern=[[1, SLOTS + 1]], base=0, channel_multiplier=0, allow_small_or_imprecise_dtypes=True))
            assert n == CONSTS
            pool.memset(kvrow[:, :, :, :, KBLK * HD:KROW].rearrange("p b h t c -> p (b h t) c"), 1.0).then_inc(ones_set, 1)

            def store_k(u, a, k, first, last):
                pool.wait_ge(kT_ready, 2 * u + 2)
                pool.dma_start(kst_d[:, :, bass.ds(u * P, P)].rearrange("h r n -> r h n"), kTbuf[a][0:K3]).then_inc(kst_stored[a], 16)

            sweep(pool, NC, store_k)
            pool.wait_ge(v_step, 1)
            pool.partition_all_reduce(svrow, vam, P, bass.bass_isa.ReduceOp.absmax).then_inc(vmax_ready, 1)

            pool.wait_ge(v_step, V_STEPS)
            for a in range(2):
                pool.wait_ge(kst_stored[a], 16 * (NC // 2))
            for a in range(2):
                pool.memset(kA[a][K3:K3 + 3, :], 1.0).then_inc(ones_set, 1)

            pool.wait_ge(att_added, NT)
            pool.memset(zero, 0.0).then_inc(zero_made, 1)
            pool.wait_ge(r_step, R_STEPS)
            pool.wait_ge(xs_zeroed, 16 * SLOTS)
            for t in range(NT):
                for j in range(2):
                    pool.indirect_dma_start(xs_d, bass.IndirectOffsetOnAxis(ap=posi[:, j, t:t + 1], axis=0), xn[:, t, :], None).then_inc(scattered, 16)
            def store_y(u, a, k, first, last):
                pool.wait_ge(y_ready, at(u))
                pool.dma_start(ys_d[bass.ds(u * P, P), :], yb[a]).then_inc(y_stored[a], 16)

            sweep(pool, SLOTS, store_y)
            for a, m in ((0, (SLOTS + 1) // 2), (1, SLOTS // 2)):
                pool.wait_ge(y_stored[a], 16 * m)
            for t in range(NT):
                for j in range(2):
                    pool.indirect_dma_start(grow[2 * t + j], None, ys_d, bass.IndirectOffsetOnAxis(ap=posi[:, j, t:t + 1], axis=0)).then_inc(gathered[t], 16)

            def store_q(u, a, k, first, last):
                pool.wait_ge(qT_ready, 2 * u + 2)
                pool.dma_start(qst_d[:, :, bass.ds(u * P, P)].rearrange("h r n -> r h n"), qTbuf[a][0:K3]).then_inc(qst_stored[a], 16)

            sweep(pool, NT, store_q)

            def stage_v(u, a, k, first, last):
                if first:
                    pool.wait_ge(moe_added, 2 * NT)
                else:
                    pool.wait_ge(av_done, 8 * (u - 1))
                pool.tensor_copy(vhead[a], vint[:, :, bass.ds(u * HD, HD)]).then_inc(v_staged, 1)

            sweep(pool, H, stage_v)

            for w in range(3):
                pool.wait_ge(fw_sum, w + 1)
                pool.partition_all_reduce(wst[:, 3 + w:4 + w], wst[:, w:w + 1], P, bass.bass_isa.ReduceOp.add).then_inc(fw_all, 1)

        @block.tensor
        def _(pe):
            pe.wait_ge(consts_made, CONSTS)

            def turn_k(u, a):
                pe.wait_ge(krow_ready, at(u))
                pe.wait_ge(kT_ready, 2 * u)
                for g, bank in enumerate((bank4, bank5)):
                    view = bank[:].bitcast(BF16)
                    for h in range(8):
                        ins = pe.transpose(view[0:K3, h * P:(h + 1) * P],
                                           krow[a][:, 8 * g + h].rearrange("p c d -> p (c d)"), idb)
                    ins.then_inc(k_turned, 1)

            def kv_tile(u, a, k, first, last):
                pe.wait_ge(ctx_loaded[a], 16 * (k + 1))
                if not first:
                    pe.wait_ge(ctxT_ready, at(u - 1))
                for c in range(KC):
                    ins = pe.transpose(bank6[:, c * P:(c + 1) * P], cin[a][:, c * P:(c + 1) * P], idf)
                ins.then_inc(ctx_turned, 1)
                if not first:
                    turn_k(u - 1, 1 - a)
                pe.wait_ge(ctxT_ready, at(u))
                if first:
                    pe.wait_ge(wkv_loaded, 32)
                else:
                    pe.wait_ge(kf_done, at(u - 1))
                for c in range(KC):
                    ins = pe.matmul(scores[:, 0:D], cT[a][:, c], wkv[:, c, 0:D], start=c == 0, stop=c == KC - 1)
                ins.then_inc(k_proj, 1)
                if not first:
                    pe.wait_ge(vf_done, at(u - 1))
                for c in range(KC):
                    ins = pe.matmul(scores[:, D:2 * D], cT[a][:, c], wkv[:, c, D:2 * D], start=c == 0, stop=c == KC - 1)
                ins.then_inc(v_proj, 1)
                if last:
                    turn_k(u, a)

            sweep(pe, NC, kv_tile)

            def prep_turn(what, u, b, first):
                view = bank6[:].bitcast(BF16)
                if what == "ka":
                    pe.wait_ge(staged, 2 * u + 2)
                    if first:
                        pe.wait_ge(ctxT_ready, at(NC - 1))
                    else:
                        pe.wait_ge(m_ready, at(u - 1))
                    for t in range(KT):
                        ins = pe.transpose(view[0:K3, t * P:(t + 1) * P], kst[b][:, t, 0:K3], idb)
                    ins.then_inc(ka_turned, 1)
                elif what == "kb":
                    pe.wait_ge(ka_ready, at(u))
                    for t in range(KT):
                        ins = pe.transpose(view[0:K3, t * P:(t + 1) * P], kst[b][:, t, HD:HD + K3], idb)
                    ins.then_inc(kb_turned, 1)
                elif what == "q":
                    pe.wait_ge(kb_ready, at(u))
                    for g in range(2):
                        for t in range(QT):
                            ins = pe.transpose(view[0:K3, (g * QT + t) * P:(g * QT + t + 1) * P],
                                               qst[b][:, t, 2 * g * HD:2 * g * HD + K3], idb)
                    ins.then_inc(q_turned, 1)

            def smax(u, b, t):
                s = 1024 * (t % 2)
                if t == 0:
                    pe.wait_ge(qab_ready, at(u))
                if not (isinstance(u, int) and u == 0 and t < 2):
                    pe.wait_ge(max_done, QT * u + t - 1)
                q = qAB[b][0:K3, 0, t * P:(t + 1) * P]
                pe.matmul(scores[:, s:s + 512], q, kA[b][0:K3, 0:512], start=True, stop=True)
                n = (t + 1) * P
                pe.matmul(scores[:, s + 512:s + 512 + n], q, kA[b][0:K3, 512:512 + n], start=True, stop=False)
                pe.matmul(scores[:, s + 512 + n - P:s + 512 + n], idb, mask_q, start=False, stop=True).then_inc(smax_done, 1)

            def turn_m(u, b):
                pe.wait_ge(m_step, 4 * u + 4)
                view = bank6[:].bitcast(BF16)
                for t in range(QT):
                    ins = pe.transpose(view[K3:K3 + 3, t * P:(t + 1) * P], mparts[:, t, 0:3], idb)
                ins.then_inc(m_turned, 1)

            def st(u, a, k, first):
                if k == 0:
                    pe.wait_ge(m_ready, at(u))
                if not (first and k < 2):
                    pe.wait_ge(exp_done, KT * u + k - 1)
                else:
                    pe.wait_ge(kT_ready, 2 * NC)
                bank = (bank4, bank5)[k % 2]
                w = WID[k]
                diag = k >= HALF
                pe.matmul(bank[:, 0:w], kA[a][0:K3 + 3, k * P:(k + 1) * P], qAB[a][0:K3 + 3, 0, SQ - w:SQ], start=True, stop=False)
                ins = pe.matmul(bank[:, 0:w], kB[a][0:K3, k * P:(k + 1) * P], qAB[a][0:K3, 1, SQ - w:SQ], start=False, stop=not diag)
                if diag:
                    ins = pe.matmul(bank[:, 0:P], idb, mask_k, start=False, stop=True)
                ins.then_inc(st_done, 1)

            def pv(u, a, k, first):
                if k == 0 and not first:
                    pe.wait_ge(rl_done, at(u - 1))
                if k % 2 == 0:
                    pe.wait_ge(p2_done, 4 * u + k // 2 + 1)
                    pe.wait_ge(p1_done, 4 * u + k // 2 + 1)
                for t in range(max(0, k - HALF), QT):
                    c = OFF[k] + (t * P - (SQ - WID[k]))
                    for part in (p1, p2):
                        ins = pe.matmul(bank7[:, t * 97:t * 97 + 97], part[:, c:c + P], kst[a][:, k, HD:HD + 97],
                                        start=(k == 0 and t == 0 and part is p1), stop=(k == KT - 1 and t == QT - 1 and part is p2),
                                        skip_group_check=True)
                if k == KT - 1:
                    ins.then_inc(pv_done, 1)

            def att_unit(u, a, k, first, last):
                b = 1 - a
                if not last:
                    prep_turn("ka", u + 1, b, False)
                st(u, a, 0, first); st(u, a, 1, first)
                if not last:
                    prep_turn("kb", u + 1, b, False)
                st(u, a, 2, first); st(u, a, 3, first)
                if not last:
                    prep_turn("q", u + 1, b, False)
                st(u, a, 4, first); st(u, a, 5, first)
                if not last:
                    smax(u + 1, b, 0); smax(u + 1, b, 1)
                st(u, a, 6, first); st(u, a, 7, first)
                if not last:
                    smax(u + 1, b, 2); smax(u + 1, b, 3)
                for j in range(KT):
                    pv(u, a, j, first)
                if not last:
                    turn_m(u + 1, b)

            for what in ("ka", "kb", "q"):
                prep_turn(what, 0, 0, True)
            pe.wait_ge(vf_done, NC)
            pe.wait_ge(ones_set, 3)
            for t in range(QT):
                smax(0, 0, t)
            turn_m(0, 0)
            sweep(pe, UNITS, att_unit)

            pe.wait_ge(gw_loaded, 16)
            pe.wait_ge(m_ready, UNITS)
            pe.wait_ge(exp_done, UNITS * KT)
            pe.wait_ge(rl_done, UNITS)
            for c in range(KC):
                ins = pe.transpose(bank6[:, c * E:(c + 1) * E], gw[0:E, c * P:(c + 1) * P], idf[0:E, 0:E])
            ins.then_inc(gw_turned, 1)
            turn_rows(pe, xn, ln_step, LN_STEPS * 2 - NT, xn_turned, xT_ready, (bank4, bank5), idf)
            pe.wait_ge(gwT_ready, 1)
            pe.wait_ge(xT_ready, NT)
            for t in range(NT):
                for c in range(KC):
                    ins = pe.matmul(bank7[:, t * E:(t + 1) * E], XT[:, c, t * P:(t + 1) * P], gwT[:, c], start=c == 0, stop=c == KC - 1)
            ins.then_inc(logits_done, 1)
            pe.wait_ge(r_step, R_ASSIGNED)
            pe.wait_ge(gwT_ready, 1)
            flat = asg.rearrange("p t e -> p (t e)")
            pe.matmul(bank6[:, 0:NT * E], tri, flat, start=True, stop=False, skip_group_check=True)
            for s in range(1, NT):
                pe.matmul(bank6[:, s * E:NT * E], ones, flat[:, 0:(NT - s) * E], start=False, stop=s == NT - 1, skip_group_check=True)
            for t in range(NT):
                ins = pe.matmul(bank7[:, 128:128 + E], ones, asg[:, t], start=t == 0, stop=t == NT - 1)
            ins.then_inc(ranks_done, 1)

            def turn_slot(u, a, k):
                pe.wait_ge(xs_loaded[a], 16 * (k + 1))
                for c in range(KC):
                    ins = pe.transpose(bank6[:, c * P:(c + 1) * P], xsin[a][:, c * P:(c + 1) * P], idf)
                ins.then_inc(xs_turned, 1)

            def slot(u, a, k, first, last):
                wa, wb = wbuf[a]
                if first:
                    turn_slot(0, 0, 0)
                pe.wait_ge(xsT_ready, at(u))
                pe.wait_ge(w_loaded[a], 48 * (k + 1))
                for half in range(2):
                    if not first:
                        pe.wait_ge(h_done, 2 * (u - 1) + half + 1)
                    for m in range(2):
                        for c in range(KC):
                            ins = pe.matmul(scores[:, m * 1024 + half * 512:m * 1024 + half * 512 + 512], xsT[a][:, c],
                                            wa[:, m, c, half * 512:half * 512 + 512], start=c == 0, stop=c == KC - 1)
                    ins.then_inc(up_done, 1)
                if not last:
                    turn_slot(u + 1, 1 - a, k + a)
                for half, bank in enumerate((bank4, bank5)):
                    pe.wait_ge(h_done, 2 * u + half + 1)
                    for c in range(4):
                        ins = pe.transpose(bank[:, c * P:(c + 1) * P], hb[:, (4 * half + c) * P:(4 * half + c + 1) * P], idf)
                    ins.then_inc(h_turned, 1)
                for half, ready in enumerate((hT0_ready, hT1_ready)):
                    pe.wait_ge(ready, at(u))
                    if half == 0 and not first:
                        pe.wait_ge(y_ready, at(u - 1))
                    for c in range(4 * half, 4 * half + 4):
                        ins = pe.matmul(bank7[:, :], hT[:, c], wb[:, c], start=c == 0, stop=c == EC - 1)
                ins.then_inc(y_done, 1)

            sweep(pe, SLOTS, slot)

            pe.wait_ge(hT0_ready, SLOTS)
            pe.wait_ge(hT1_ready, SLOTS)
            pe.wait_ge(y_ready, SLOTS)
            turn_rows(pe, xn3, ln_step, LN_STEPS * 3 - NT, x3_turned, x3T_ready, (bank4, bank5), idf)

            def turn_q(u, a, first):
                pe.wait_ge(q3_ready, at(u))
                if not first:
                    pe.wait_ge(qT_ready, 2 * u)
                for g, bank in enumerate((bank4, bank5)):
                    view = bank[:].bitcast(BF16)
                    for h in range(8):
                        ins = pe.transpose(view[0:K3, h * P:(h + 1) * P],
                                           q3row[a][:, 8 * g + h].rearrange("p c d -> p (c d)"), idb)
                    ins.then_inc(q3_turned, 1)

            pe.wait_ge(x3T_ready, NT)
            pe.wait_ge(wq_loaded, 32)

            def q_tile(u, a, k, first, last):
                if not first:
                    pe.wait_ge(qf_done, at(u - 1))
                for c in range(KC):
                    ins = pe.matmul(bank7[:, :], XT3[:, c, bass.ds(u * P, P)], wq_sb[:, c, :], start=c == 0, stop=c == KC - 1)
                ins.then_inc(q_proj, 1)
                turn_q(u, a, first)

            for u in range(NT):
                q_tile(u, u % 2, u // 2, u == 0, False)

            def a1_scores(h, a, t, first):
                for half in range(2):
                    if not first:
                        pe.wait_ge(s_read, 2 * (8 * h + t) + half - 1)
                    for j in range(2):
                        s = half * 1024 + j * 512
                        ins = pe.matmul(scores[:, s:s + 512], qhead[a][0:K3, t * P:(t + 1) * P], khead[a][0:K3, s:s + 512], start=True, stop=True)
                    ins.then_inc(s_done, 1)

            def a1_turn(h, a, t, first):
                i = t % 2
                pe.wait_ge(p_ready, 8 * h + t + 1)
                for g, (bank, copied) in enumerate(((bank4, pT_lo), (bank5, pT_hi))):
                    if not first:
                        pe.wait_ge(copied, 8 * h + t)
                    else:
                        pe.wait_ge(qT_ready, 2 * NT)
                    view = bank[:].bitcast(BF16)
                    for c in range(8):
                        ins = pe.transpose(view[:, c * P:(c + 1) * P], p16[i][:, (8 * g + c) * P:(8 * g + c + 1) * P].bitcast(BF16), idb)
                    ins.then_inc(p_turned, 1)

            def a1_pv(h, a, t, first):
                i = t % 2
                bank = (bank6, bank7)[a]
                pe.wait_ge(pT_lo, 8 * h + t + 1)
                pe.wait_ge(pT_hi, 8 * h + t + 1)
                if t == 0:
                    pe.wait_ge(v_staged, at(h))
                    if not first:
                        pe.wait_ge(a_post, 3 * (h - 1))
                for c in range(NC):
                    ins = pe.matmul(bank[:, t * HD:(t + 1) * HD], pT[i][:, c], vhead[a][:, c], start=c == 0, stop=c == NC - 1)
                ins.then_inc(av_done, 1)

            def a1_head(h, a, k, first, last):
                for t in range(NT):
                    if t < NT - 2:
                        a1_scores(h, a, t + 2, False)
                    elif not last:
                        if t == NT - 2:
                            pe.wait_ge(k_loaded[1 - a], 32 * (k + a + 1))
                        a1_scores(h + 1, 1 - a, t + 2 - NT, False)
                    a1_turn(h, a, t, first and t == 0)
                    if t > 0:
                        a1_pv(h, a, t - 1, first)
                    elif not first:
                        a1_pv(h - 1, 1 - a, NT - 1, False)
                if last:
                    a1_pv(h, a, NT - 1, False)

            pe.wait_ge(qf_done, NT)
            pe.wait_ge(h_done, 2 * SLOTS)
            pe.wait_ge(k_loaded[0], 32)
            a1_scores(0, 0, 0, True)
            a1_scores(0, 0, 1, False)
            sweep(pe, H, a1_head)

            for t in range(NT):
                pe.wait_ge(a_post, 3 * H)
                if t >= 2:
                    pe.wait_ge(oT_ready, t - 1)
                else:
                    pe.wait_ge(pT_lo, 8 * H)
                    pe.wait_ge(pT_hi, 8 * H)
                bank = (bank4, bank5)[t % 2]
                for c in range(KC):
                    ins = pe.transpose(bank[:, c * P:(c + 1) * P], oh[:, t, c * P:(c + 1) * P], idf)
                ins.then_inc(o_turned, 1)
            pe.wait_ge(wp_loaded, 32)
            for t in range(NT):
                pe.wait_ge(oT_ready, at(t))
                bank = (bank6, bank7)[t % 2]
                if t >= 2:
                    pe.wait_ge(o_added, 2 * (t - 2) + 1)
                for c in range(KC):
                    ins = pe.matmul(bank[:, :], XT3[:, c, t * P:(t + 1) * P], wp_sb[:, c, :], start=c == 0, stop=c == KC - 1)
                ins.then_inc(o_proj, 1)

            g = 0
            for w in range(3):
                pe.wait_ge(fw_int, 2 * w + 2)
                rows = wint if w < 2 else wint.rearrange("p (o c) n -> p o (c n)", o=KC)
                for o in range(FC if w < 2 else KC):
                    cols = KC if w < 2 else FC
                    for c0 in range(0, cols, 8 if w == 2 else 4):
                        bank = (bank4, bank5)[g % 2]
                        if g >= 2:
                            pe.wait_ge(fwT_ready, g - 1)
                        else:
                            pe.wait_ge(oT_ready, NT)
                        view = bank[:].bitcast(BF16)
                        for c in range(8 if w == 2 else 4):
                            ins = pe.transpose(view[:, c * P:(c + 1) * P], rows[:, o, (c0 + c) * P:(c0 + c + 1) * P], idb)
                        ins.then_inc(fw_turned, 1)
                        g += 1
            for t in range(NT):
                pe.wait_ge(f_step, F_STEPS_Q)
                bank = (bank6, bank7)[t % 2]
                if t >= 2:
                    pe.wait_ge(x4T_ready, t - 1)
                else:
                    pe.wait_ge(o_added, 2 * NT)
                view = bank[:].bitcast(BF16)
                for c in range(KC):
                    ins = pe.transpose(view[:, c * P:(c + 1) * P], xq4[:, t, c * P:(c + 1) * P], idb)
                ins.then_inc(x4_turned, 1)
            pe.wait_ge(fwT_ready, FW_GROUPS)
            pe.wait_ge(x4T_ready, NT)
            for t in range(NT):
                for q in range(4):
                    n = 4 * t + q
                    for w, bank in ((0, scores[:, (q % 4) * 512:(q % 4) * 512 + 512]), (1, (bank4, bank5)[q % 2][:, :])):
                        if w == 0 and t > 0:
                            pe.wait_ge(fsilu_done, n - 3)
                        if w == 1 and n >= 2:
                            pe.wait_ge(fh_done, n - 1)
                        for c in range(KC):
                            ins = pe.matmul(bank, xT4[:, c, t * P:(t + 1) * P], wT[w][:, c, q * 512:(q + 1) * 512], start=c == 0, stop=c == KC - 1)
                        ins.then_inc(gu_done, 1)
            for t in range(NT):
                pe.wait_ge(f2_step, 2 * t + 2)
                for g, bank in enumerate((bank4, bank5)):
                    if t:
                        pe.wait_ge(fhT_ready, 2 * (t - 1) + g + 1)
                    view = bank[:].bitcast(BF16)
                    for c in range(8):
                        ins = pe.transpose(view[:, c * P:(c + 1) * P], hqr[:, (8 * g + c) * P:(8 * g + c + 1) * P], idb)
                    ins.then_inc(fh_turned, 1)
                pe.wait_ge(fhT_ready, 2 * t + 2)
                bank = (bank6, bank7)[t % 2]
                if t >= 2:
                    pe.wait_ge(fout_done, t - 1)
                for c in range(FC):
                    ins = pe.matmul(bank[:, :], hqT[:, c], wdT[:, c], start=c == 0, stop=c == FC - 1)
                ins.then_inc(fdown_done, 1)

        @block.scalar
        def _(act):
            def kv_tile(u, a, k, first, last):
                act.wait_ge(ctx_turned, at(u))
                act.activation(cT[a].rearrange("p c n -> p (c n)"), bank6[:, :], ACT.Copy).then_inc(ctxT_ready, 1)
                act.wait_ge(ctx_loaded[a], 16 * (k + 1))
                if first:
                    act.wait_ge(ones_set, 1)
                parts = context_parts(u)
                act.activation(parts[:, :, 0:3:2], cin[a].rearrange("p (h o d) -> p h o d", h=H, o=1).broadcast_to([P, H, 2, HD]),
                               ACT.Copy).then_inc(c1_done, 1)
                act.wait_ge(cr_done, at(u))
                act.activation(parts[:, :, 1], by_head(cr), ACT.Copy).then_inc(c2_done, 1)
                if not first:
                    copy_kT(u - 1, 1 - a, k - 1 + a)
                act.wait_ge(kd_done, at(u))
                act.activation(krow[a][:, :, 0], kd, ACT.Copy).then_inc(kq1_done, 1)
                act.wait_ge(kqr_done, at(u))
                act.activation(krow[a][:, :, 1], kqr, ACT.Copy).then_inc(kq2_done, 1)
                if last:
                    copy_kT(u, a, k)

            def copy_kT(u, a, k):
                act.wait_ge(kst_stored[a], 16 * k)
                for g, bank in enumerate((bank4, bank5)):
                    act.wait_ge(k_turned, 2 * u + g + 1)
                    act.activation(kTbuf[a][0:K3, 8 * g:8 * g + 8].rearrange("p h n -> p (h n)"),
                                   bank[:].bitcast(BF16)[0:K3, :], ACT.Copy).then_inc(kT_ready, 1)

            act.preload_act_table(ACT.Copy)
            sweep(act, NC, kv_tile)

            def std(n):
                act.wait_ge(ln_var, n)
                act.activation(std0, ln_t[:, 0], ACT.Sqrt).then_inc(ln_std, 1)

            std(1)
            for b in range(B):
                act.wait_ge(ln_step, LN_STEPS - NT + (b + 1) * QT)
                rows = xn0[:, b * QT:(b + 1) * QT].rearrange("p t (h d) -> p t h d", h=H)
                parts = qrow[:, b].rearrange("p h t (c d) -> p t h c d", d=HD)
                for blk in (0, 1, 4):
                    act.activation(parts[:, :, :, blk], rows, ACT.Copy).then_inc(qs1, 1)
                act.wait_ge(qs_r, b + 1)
                act.activation(parts[:, :, :, 2], qr[:, b * QT:(b + 1) * QT].rearrange("p t (h d) -> p t h d", h=H), ACT.Copy).then_inc(qs2, 1)

            def copy_turned(u, b, turned, dst, ready):
                act.wait_ge(turned, at(u))
                act.activation(dst[b][0:K3, :], bank6[:].bitcast(BF16)[0:K3, :], ACT.Copy).then_inc(ready, 1)

            def copy_m(u, b):
                act.wait_ge(m_turned, at(u))
                act.activation(qAB[b][K3:K3 + 3, 0, :], bank6[:].bitcast(BF16)[K3:K3 + 3, 0:SQ], ACT.Copy).then_inc(m_ready, 1)

            def att_unit(u, a, k, first, last):
                b = 1 - a
                for g in range(4):
                    for j in (2 * g, 2 * g + 1):
                        if j == 2 * g and not first:
                            act.wait_ge(p2_done, 4 * (u - 1) + g + 1)
                        act.wait_ge(st_done, KT * u + j + 1)
                        act.activation(eP[:, OFF[j]:OFF[j] + WID[j]], (bank4, bank5)[j % 2][:, 0:WID[j]], ACT.Exp, scale=SCALE).then_inc(exp_done, 1)
                    if g == 0 and not first:
                        act.wait_ge(pv_done, at(u - 1))
                    act.wait_ge(exp_done, KT * u + 2 * g + 2)
                    s, e = OFF[2 * g], OFF[2 * g + 1] + WID[2 * g + 1]
                    act.activation(p1[:, s:e], eP[:, s:e], ACT.Copy).then_inc(p1_done, 1)
                    if g == 0 and not last:
                        copy_turned(u + 1, b, ka_turned, kA, ka_ready)
                    if g == 1 and not last:
                        copy_turned(u + 1, b, kb_turned, kB, kb_ready)
                if not last:
                    copy_m(u + 1, b)

            act.preload_act_table(ACT.Exp)
            copy_turned(0, 0, ka_turned, kA, ka_ready)
            copy_turned(0, 0, kb_turned, kB, kb_ready)
            copy_m(0, 0)
            sweep(act, UNITS, att_unit)

            def copy_rows(dst, turned, ready, banks):
                for t in range(NT):
                    act.wait_ge(turned, at(t))
                    act.activation(dst[:, :, t * P:(t + 1) * P], banks[t % 2][:].rearrange("p (c n) -> p c n", c=KC), ACT.Copy).then_inc(ready, 1)

            std(2)
            copy_rows(XT, xn_turned, xT_ready, (bank4, bank5))
            act.wait_ge(r_step, 2)
            act.activation(r8[1], r8[0], ACT.Exp).then_inc(r_exp, 1)

            def slot(u, a, k, first, last):
                for half in range(2):
                    if not first:
                        act.wait_ge(h_done, 2 * (u - 1) + half + 1)
                    act.wait_ge(up_done, 2 * u + half + 1)
                    act.activation(sg[:, half * 512:half * 512 + 512], scores[:, half * 512:half * 512 + 512], ACT.Silu).then_inc(silu_done, 1)
                act.wait_ge(h_turned, 2 * u + 1)
                act.activation(hT[:, 0:4].rearrange("p c n -> p (c n)"), bank4[:, :], ACT.Copy).then_inc(hT0_ready, 1)
                act.wait_ge(y_stored[a], 16 * k)
                act.wait_ge(y_done, at(u))
                act.activation(yb[a], bank7[:, :], ACT.Copy).then_inc(y_ready, 1)

            act.preload_act_table(ACT.Silu)
            sweep(act, SLOTS, slot)

            std(3)
            copy_rows(XT3, x3_turned, x3T_ready, (bank4, bank5))
            for u in range(NT):
                act.wait_ge(qst_stored[u % 2], 16 * (u // 2))
                for g, bank in enumerate((bank4, bank5)):
                    act.wait_ge(q3_turned, 2 * u + g + 1)
                    act.activation(qTbuf[u % 2][0:K3, 8 * g:8 * g + 8].rearrange("p h n -> p (h n)"),
                                   bank[:].bitcast(BF16)[0:K3, :], ACT.Copy).then_inc(qT_ready, 1)

            def exp_tile(h, a, t, first):
                i, n = t % 2, 8 * h + t
                if not (first and t < 2):
                    act.wait_ge(p_turned, 2 * n - 2)
                if t == 0 and not first:
                    act.wait_ge(a_post, 3 * (h - 1))
                act.wait_ge(bias_ready, n + 1)
                act.activation(p16[i], ssb[i], ACT.Exp, bias=ebias[i], scale=-1.0, accum_out=rsum[a][:, t:t + 1]).then_inc(p_ready, 1)

            def a1_head(h, a, k, first, last):
                for t in range(NT):
                    if t < NT - 1:
                        exp_tile(h, a, t + 1, first)
                    elif not last:
                        exp_tile(h + 1, 1 - a, 0, False)
                    act.wait_ge(p_turned, 2 * (8 * h + t) + 2)
                    act.activation(pT[t % 2][:, 8:16].rearrange("p c n -> p (c n)"), bank5[:].bitcast(I16), ACT.Copy).then_inc(pT_hi, 1)

            act.preload_act_table(ACT.Exp)
            exp_tile(0, 0, 0, True)
            sweep(act, H, a1_head)

            copy_rows(XT3, o_turned, oT_ready, (bank4, bank5))

            g = 0
            for w in range(3):
                for o in range(FC if w < 2 else KC):
                    for c0 in range(1 if w < 2 else 2):
                        act.wait_ge(fw_turned, at(g))
                        bank = (bank4, bank5)[g % 2][:].bitcast(BF16)
                        if w < 2:
                            act.activation(wT[w][:, :, o * P:(o + 1) * P], bank[:, 0:KC * P].rearrange("p (c n) -> p c n", c=KC), ACT.Copy).then_inc(fwT_ready, 1)
                        else:
                            act.activation(wdT[:, 8 * c0:8 * c0 + 8, o * P:(o + 1) * P], bank.rearrange("p (c n) -> p c n", c=8), ACT.Copy).then_inc(fwT_ready, 1)
                        g += 1
            std(4)
            for t in range(NT):
                act.wait_ge(x4_turned, at(t))
                act.activation(xT4[:, :, t * P:(t + 1) * P], (bank6, bank7)[t % 2][:].bitcast(BF16)[:, 0:KC * P].rearrange("p (c n) -> p c n", c=KC),
                               ACT.Copy).then_inc(x4T_ready, 1)
            for t in range(NT):
                for q in range(4):
                    n = 4 * t + q
                    act.wait_ge(gu_done, 2 * n + 1)
                    if n >= 4:
                        act.wait_ge(fh_done, n - 3)
                    act.activation(sgb[:, q * 512:(q + 1) * 512], scores[:, q * 512:(q + 1) * 512], ACT.Silu, scale=gscale[:, 0, t:t + 1]).then_inc(fsilu_done, 1)
                act.wait_ge(fh_done, 4 * t + 4)
                if t:
                    act.wait_ge(fsq_done, t)
                act.activation(hqr, hball[:, t], ACT.Square, accum_out=ssq[:, t:t + 1]).then_inc(fsq_done, 1)
            act.wait_ge(f_var, 1)
            act.activation(std0, fsm[:, 0], ACT.Sqrt).then_inc(f_std, 1)
            for t in range(NT):
                for g, bank in enumerate((bank4, bank5)):
                    act.wait_ge(fh_turned, 2 * t + g + 1)
                    act.activation(hqT[:, 8 * g:8 * g + 8].rearrange("p c n -> p (c n)"), bank[:].bitcast(BF16), ACT.Copy).then_inc(fhT_ready, 1)

        @block.vector
        def _(dve):
            def kv_tile(u, a, k, first, last):
                parts = context_parts(u)
                dve.wait_ge(c1_done, at(u))
                if not first:
                    dve.wait_ge(c3_done, at(u - 1))
                dve.tensor_tensor(by_head(cr), by_head(cin[a]), parts[:, :, 0], ALU.subtract).then_inc(cr_done, 1)
                dve.wait_ge(k_proj, at(u))
                if first:
                    dve.wait_ge(wkv_loaded, 32)
                dve.tensor_tensor(kf.rearrange("p h d -> p (h d)"), scores[:, 0:D], bkv_row[:, 0:D], ALU.add).then_inc(kf_done, 1)
                dve.wait_ge(v_proj, at(u))
                dve.tensor_tensor(vf[:, bass.ds(u, 1)].rearrange("p u d -> p (u d)"), scores[:, D:2 * D], bkv_row[:, D:2 * D], ALU.add).then_inc(vf_done, 1)
                dve.wait_ge(kf_done, at(u))
                dve.tensor_reduce(kam, kf, X, ALU.max, apply_absolute_value=True).then_inc(kam_done, 1)
                dve.wait_ge(kam_done, at(u))
                dve.tensor_scalar(ks, kam, 1.0 / 127.0, 1e-8, ALU.mult, ALU.max).then_inc(ks_done, 1)
                dve.wait_ge(ks_done, at(u))
                dve.reciprocal(kinv, ks).then_inc(kinv_done, 1)
                dve.wait_ge(kinv_done, at(u))
                dve.tensor_tensor(kx, kf, each(kinv, [H, HD]), ALU.mult).then_inc(kx_done, 1)
                dve.wait_ge(kx_done, at(u))
                dve.tensor_scalar(kr, kx, MAGIC, MAGIC, ALU.add, ALU.subtract).then_inc(kr_done, 1)
                dve.wait_ge(kr_done, at(u))
                dve.tensor_tensor(kd, kr, each(ks, [H, HD]), ALU.mult).then_inc(kd_done, 1)
                dve.wait_ge(c2_done, at(u))
                dve.tensor_tensor(parts[:, :, 3], by_head(cr), parts[:, :, 1], ALU.subtract).then_inc(c3_done, 1)
                dve.wait_ge(kq1_done, at(u))
                dve.wait_ge(kd_done, at(u))
                dve.tensor_tensor(kqr, kd, krow[a][:, :, 0], ALU.subtract).then_inc(kqr_done, 1)
                dve.wait_ge(kq2_done, at(u))
                dve.wait_ge(kqr_done, at(u))
                dve.tensor_tensor(krow[a][:, :, 2], kqr, krow[a][:, :, 1], ALU.subtract).then_inc(krow_ready, 1)

            sweep(dve, NC, kv_tile)
            dve.wait_ge(vf_done, NC)
            dve.tensor_reduce(vam, vf.rearrange("p t d -> p d t"), X, ALU.max, apply_absolute_value=True).then_inc(v_step, 1)
            dve.wait_ge(vmax_ready, 1)
            dve.tensor_scalar(svrow, svrow, 1.0 / 127.0, 1e-8, ALU.mult, ALU.max).then_inc(v_step, 1)
            dve.wait_ge(v_step, 2)
            vinv = kx.rearrange("p h d -> p (h d)")
            dve.reciprocal(vinv, svrow).then_inc(v_step, 1)
            dve.wait_ge(v_step, 3)
            dve.tensor_tensor(vf, vf, vinv.rearrange("p (o d) -> p o d", o=1).broadcast_to([P, NC, D]), ALU.mult).then_inc(v_step, 1)
            dve.wait_ge(v_step, 4)
            dve.tensor_scalar(vint, vf, MAGIC, MAGIC, ALU.add, ALU.subtract).then_inc(v_step, 1)

            def rsqrt(var, std, tmp, ready, step, n):
                dve.wait_ge(ready[0], ready[1])
                for ins in (lambda: dve.reciprocal(tmp[:, 1], std),
                            lambda: dve.tensor_tensor(tmp[:, 2], var, tmp[:, 1], ALU.mult),
                            lambda: dve.tensor_tensor(tmp[:, 3], tmp[:, 2], std, ALU.add),
                            lambda: dve.reciprocal(tmp[:, 4], tmp[:, 3]),
                            lambda: dve.tensor_scalar(tmp[:, 1], tmp[:, 4], 2.0, None, ALU.mult)):
                    ins().then_inc(step, 1)
                    n += 1
                    dve.wait_ge(step, n)
                return n

            def layer_norm(j, dst):
                n = LN_STEPS * j
                for t in range(NT):
                    dve.bn_stats(stats[:, t], xres[:, t]).then_inc(ln_step, 1)
                for t in range(NT):
                    dve.wait_ge(ln_step, n + t + 1)
                    dve.bn_aggr(mv[:, t], stats[:, t]).then_inc(ln_step, 1)
                n += 2 * NT
                dve.wait_ge(ln_step, n)
                dve.tensor_scalar(ln_t[:, 0], mv[:, :, 1], LN_EPS, None, ALU.add).then_inc(ln_var, 1)
                dve.wait_ge(ln_var, j + 1)
                n = rsqrt(ln_t[:, 0], std0, ln_t, (ln_std, j + 1), ln_step, n)
                dve.scalar_tensor_tensor(ln_t[:, 5], mv[:, :, 0], -1.0, ln_t[:, 1], ALU.mult, ALU.mult).then_inc(ln_step, 1)
                n += 1
                dve.wait_ge(ln_step, n)
                for t in range(NT):
                    dve.tensor_scalar(dst[:, t], xres[:, t], ln_t[:, 1, t:t + 1], ln_t[:, 5, t:t + 1], ALU.mult, ALU.add).then_inc(ln_step, 1)
                assert n + NT == LN_STEPS * (j + 1)

            for b in range(B):
                dve.wait_ge(x_loaded[b], 16)
            for a in range(2):
                dve.wait_ge(kst_stored[a], 16 * (NC // 2))
            dve.wait_ge(v_step, V_STEPS)
            dve.wait_ge(krow_ready, NC)
            layer_norm(0, xn0)
            for b in range(B):
                s = slice(b * QT, (b + 1) * QT)
                rows = xn0[:, s].rearrange("p t (h d) -> p t h d", h=H)
                rest = qr[:, s].rearrange("p t (h d) -> p t h d", h=H)
                parts = qrow[:, b].rearrange("p h t (c d) -> p t h c d", d=HD)
                dve.wait_ge(qs1, 3 * b + 1)
                dve.wait_ge(ln_step, LN_STEPS)
                dve.tensor_tensor(rest, rows, parts[:, :, :, 0], ALU.subtract).then_inc(qs_r, 1)
                dve.wait_ge(qs2, b + 1)
                dve.wait_ge(qs_r, b + 1)
                dve.tensor_tensor(parts[:, :, :, 3], rest, parts[:, :, :, 2], ALU.subtract).then_inc(qs3, 1)
            dve.wait_ge(qs3, B)
            dve.wait_ge(qs1, 3 * B)
            dve.wait_ge(c3_done, NC)
            dve.wait_ge(c2_done, NC)

            def stage(u, b):
                dve.tensor_copy(kst[b].rearrange("p t c -> p (t c)"),
                                kvrow.rearrange("p b h t c -> p (b h) (t c)")[:, bass.ds(u, 1)].rearrange("p u c -> p (u c)")).then_inc(staged, 1)
                dve.tensor_copy(qst[b].rearrange("p t c -> p (t c)"),
                                qrow.rearrange("p b h t c -> p (b h) (t c)")[:, bass.ds(u, 1)].rearrange("p u c -> p (u c)")).then_inc(staged, 1)

            def copy_q(u, b):
                dve.wait_ge(q_turned, at(u))
                dve.tensor_copy(qAB[b][0:K3].rearrange("p g n -> p (g n)"), bank6[:].bitcast(BF16)[0:K3, :]).then_inc(qab_ready, 1)

            def take_max(u, t):
                s = 1024 * (t % 2)
                dve.wait_ge(smax_done, QT * u + t + 1)
                dve.reduce_max(mx[:, t:t + 1], scores[:, s:s + 512 + (t + 1) * P], X).then_inc(max_done, 1)

            def split_m(u, first):
                dve.wait_ge(max_done, QT * u + QT)
                if not first:
                    dve.wait_ge(m_turned, at(u - 1))
                dve.tensor_scalar(mparts[:, :, 0], mx, -1.0, None, ALU.mult).then_inc(m_step, 1)
                dve.wait_ge(m_step, 4 * u + 1)
                dve.scalar_tensor_tensor(mr, mx, -1.0, mparts[:, :, 0], ALU.mult, ALU.subtract).then_inc(m_step, 1)
                dve.wait_ge(m_step, 4 * u + 2)
                dve.tensor_copy(mparts[:, :, 1], mr).then_inc(m_step, 1)
                dve.wait_ge(m_step, 4 * u + 3)
                dve.tensor_tensor(mparts[:, :, 2], mr, mparts[:, :, 1], ALU.subtract).then_inc(m_step, 1)

            def rest_of_p(u, g):
                s, e = OFF[2 * g], OFF[2 * g + 1] + WID[2 * g + 1]
                dve.wait_ge(p1_done, 4 * u + g + 1)
                dve.tensor_tensor(p2[:, s:e], eP[:, s:e], p1[:, s:e], ALU.subtract).then_inc(p2_done, 1)

            def finish_unit(u, first):
                dve.wait_ge(pv_done, at(u))
                if not first:
                    dve.wait_ge(o_done, at(u - 1))
                dve.tensor_reduce(osum, bank7[:, 0:4 * 97].rearrange("p (t c) -> p t c", t=QT)[:, :, 0:K3].rearrange("p t (c d) -> p t d c", d=HD),
                                  X, ALU.add).then_inc(osum_done, 1)
                dve.reciprocal(rl, bank7[:, 96:4 * 97:97]).then_inc(rl_done, 1)
                dve.wait_ge(osum_done, at(u))
                dve.wait_ge(rl_done, at(u))
                dve.tensor_tensor(oatt.rearrange("p b h t d -> p (b h) t d")[:, bass.ds(u, 1)].rearrange("p u t d -> p (u t) d"),
                                  osum, each(rl, [QT, HD]), ALU.mult).then_inc(o_done, 1)

            def att_unit(u, a, k, first, last):
                b = 1 - a
                if not first:
                    dve.wait_ge(pv_done, at(u - 1))
                if not last:
                    stage(u + 1, b)
                rest_of_p(u, 0)
                if not last:
                    copy_q(u + 1, b)
                rest_of_p(u, 1)
                if not last:
                    take_max(u + 1, 0)
                rest_of_p(u, 2)
                if not last:
                    take_max(u + 1, 1)
                rest_of_p(u, 3)
                if not last:
                    take_max(u + 1, 2)
                    take_max(u + 1, 3)
                    split_m(u + 1, False)
                finish_unit(u, first)

            stage(0, 0)
            copy_q(0, 0)
            for t in range(QT):
                take_max(0, t)
            split_m(0, True)
            sweep(dve, UNITS, att_unit)
            dve.wait_ge(o_done, UNITS)
            for t in range(NT):
                dve.tensor_tensor(by_head(xres[:, t]), by_head(xres[:, t]), oatt[:, t // QT, :, t % QT], ALU.add).then_inc(att_added, 1)
            dve.wait_ge(att_added, NT)

            layer_norm(1, xn)
            dve.wait_ge(gw_turned, 1)
            dve.tensor_copy(gwT.rearrange("p c e -> p (c e)"), bank6[:, 0:KC * E]).then_inc(gwT_ready, 1)
            n = 0

            def r(ins):
                nonlocal n
                ins.then_inc(r_step, 1)
                n += 1
                dve.wait_ge(r_step, n)

            te8 = [NT, E]
            ramp = iota_e.rearrange("p (o e) -> p o e", o=1).broadcast_to([P] + te8)
            logits = bank7[:, 0:NT * E].rearrange("p (t e) -> p t e", t=NT)
            dve.wait_ge(logits_done, 1)
            r(dve.tensor_reduce(r1[0], logits, X, ALU.max))
            r(dve.tensor_tensor(r8[0], logits, each(r1[0], te8), ALU.subtract))
            dve.wait_ge(r_exp, 1)
            r(dve.tensor_reduce(r1[1], r8[1], X, ALU.add))
            r(dve.reciprocal(r1[2], r1[1]))
            r(dve.tensor_tensor(r8[2], r8[1], each(r1[2], te8), ALU.mult))
            for left, best, cand, hot in ((2, 3, 4, 5), (6, 5, 4, 7)):
                r(dve.tensor_reduce(r1[best], r8[left], X, ALU.max))
                r(dve.tensor_tensor(r8[3], r8[left], each(r1[best], te8), ALU.is_equal))
                r(dve.scalar_tensor_tensor(r8[cand], r8[3], -100.0, ramp, ALU.mult, ALU.add))
                r(dve.tensor_reduce(r1[4], r8[cand], X, ALU.min))
                r(dve.tensor_tensor(r8[hot], r8[cand], each(r1[4], te8), ALU.is_equal))
                if hot == 5:
                    r(dve.scalar_tensor_tensor(r8[6], r8[5], -2.0, r8[2], ALU.mult, ALU.add))
            r(dve.tensor_tensor(asg, r8[5], r8[7], ALU.add))
            assert n == R_ASSIGNED
            r(dve.tensor_tensor(r1[6], r1[3], r1[5], ALU.add))
            r(dve.reciprocal(r1[7], r1[6]))
            r(dve.tensor_tensor(r1[8], r1[3], r1[7], ALU.mult))
            r(dve.tensor_tensor(r1[9], r1[5], r1[7], ALU.mult))
            dve.wait_ge(ranks_done, 1)
            r(dve.tensor_scalar(te[0], bank7[:, 128:128 + E], 1.0 / P, 127.0 / 128.0 - 0.5 + 1.0 / 256.0, ALU.mult, ALU.add))
            r(dve.tensor_scalar(te[1], te[0], MAGIC, MAGIC, ALU.add, ALU.subtract))
            r(dve.tensor_tensor_scan(te[2], ones[:, 0:E], te[1], 0.0, ALU.mult, ALU.add))
            r(dve.tensor_tensor(te[3], te[2], te[1], ALU.subtract))
            r(dve.tensor_scalar(te[4], te[3], float(P), None, ALU.mult))
            r(dve.tensor_tensor(r8[8], bank6[:, 0:NT * E].rearrange("p (t e) -> p t e", t=NT),
                                te[4].rearrange("p (o e) -> p o e", o=1).broadcast_to([P] + te8), ALU.add))
            for j, hot in ((0, 5), (1, 7)):
                r(dve.tensor_tensor(r8[9 + j], r8[hot], r8[8], ALU.mult))
                r(dve.tensor_reduce(r1[j], r8[9 + j], X, ALU.add))
            for j in range(2):
                r(dve.tensor_copy(posi[:, j], r1[j]))
            r(dve.tensor_tensor(cmp, te[2].rearrange("p (o e) -> p o e", o=1).broadcast_to([P, SLOTS + 1, E]),
                                each(iota_s, [SLOTS + 1, E]), ALU.is_le))
            r(dve.tensor_reduce(slot_f, cmp, X, ALU.add))
            r(dve.tensor_scalar(slot_e, slot_f, float(E - 1), None, ALU.min))
            assert n == R_STEPS

            def copy_slot(u, a):
                dve.wait_ge(xs_turned, at(u))
                dve.tensor_copy(xsT[a].rearrange("p c n -> p (c n)"), bank6[:, :]).then_inc(xsT_ready, 1)

            def slot(u, a, k, first, last):
                for half in range(2):
                    if not first:
                        dve.wait_ge(h_turned, 2 * (u - 1) + half + 1)
                    dve.wait_ge(silu_done, 2 * u + half + 1)
                    dve.tensor_tensor(hb[:, half * 512:half * 512 + 512], scores[:, 1024 + half * 512:1536 + half * 512],
                                      sg[:, half * 512:half * 512 + 512], ALU.mult).then_inc(h_done, 1)
                if not last:
                    copy_slot(u + 1, 1 - a)
                dve.wait_ge(h_turned, 2 * u + 2)
                dve.tensor_copy(hT[:, 4:8].rearrange("p c n -> p (c n)"), bank5[:, :]).then_inc(hT1_ready, 1)

            copy_slot(0, 0)
            sweep(dve, SLOTS, slot)
            for t in range(NT):
                dve.wait_ge(gathered[t], 32)
                for j in range(2):
                    if j:
                        dve.wait_ge(moe_added, 2 * t + 1)
                    dve.scalar_tensor_tensor(xres[:, t], grow[2 * t + j], r1[8 + j][:, t:t + 1], xres[:, t], ALU.mult, ALU.add).then_inc(moe_added, 1)
            dve.wait_ge(moe_added, 2 * NT)

            layer_norm(2, xn3)
            dve.wait_ge(wq_loaded, 32)
            n = 0

            def q(ins):
                nonlocal n
                ins.then_inc(q_step, 1)
                n += 1
                dve.wait_ge(q_step, n)

            for u in range(NT):
                a = u % 2
                dve.wait_ge(q_proj, at(u))
                dve.tensor_tensor(qf.rearrange("p h d -> p (h d)"), bank7[:, :], bq_row, ALU.add).then_inc(qf_done, 1)
                dve.wait_ge(qf_done, at(u))
                q(dve.tensor_reduce(qam, qf, X, ALU.max, apply_absolute_value=True))
                q(dve.tensor_scalar(qsv, qam, SCALE / 127.0, 1e-8, ALU.mult, ALU.max))
                q(dve.tensor_scalar(nsq[:, :, u], qsv, -1.0, None, ALU.mult))
                q(dve.reciprocal(qinv, qsv))
                q(dve.tensor_scalar(qam, qinv, SCALE, None, ALU.mult))
                q(dve.tensor_tensor(qx, qf, each(qam, [H, HD]), ALU.mult))
                if u >= 2:
                    dve.wait_ge(q3_turned, 2 * (u - 1))
                dve.tensor_scalar(q3row[a], qx.rearrange("p h (o d) -> p h o d", o=1).broadcast_to([P, H, 3, HD]), MAGIC, MAGIC,
                                  ALU.add, ALU.subtract).then_inc(q3_ready, 1)

            def read_scores(h, a, t, first):
                i, n = t % 2, 8 * h + t
                if not (first and t < 2):
                    dve.wait_ge(p_ready, n - 1)
                for half in range(2):
                    s = half * 1024
                    dve.wait_ge(s_done, 2 * n + half + 1)
                    dve.tensor_scalar(ssb[i][:, s:s + 1024], scores[:, s:s + 1024], nsq[:, bass.ds(h, 1), t], None, ALU.mult, ALU.min,
                                      accum_out=nmx[i][:, half:half + 1]).then_inc(s_read, 1)
                dve.wait_ge(s_read, 2 * n + 2)
                dve.tensor_scalar(ebias[i], nmx[i][:, 0:1], nmx[i][:, 1:2], LN255, ALU.min, ALU.add).then_inc(bias_ready, 1)

            def finish_head(h, a):
                bank = (bank6, bank7)[a]
                dve.wait_ge(av_done, 8 * (h + 1))
                dve.reciprocal(rrec, rsum[a]).then_inc(a_post, 1)
                dve.wait_ge(a_post, 3 * h + 1)
                dve.tensor_tensor(otmp, bank[:, 0:NT * HD].rearrange("p (t d) -> p t d", t=NT), each(rrec, [NT, HD]), ALU.mult).then_inc(a_post, 1)
                dve.wait_ge(a_post, 3 * h + 2)
                dve.tensor_tensor(oh[:, :, bass.ds(h * HD, HD)], otmp,
                                  svrow[:, bass.ds(h * HD, HD)].rearrange("p (o d) -> p o d", o=1).broadcast_to([P, NT, HD]), ALU.mult).then_inc(a_post, 1)

            def a1_head(h, a, k, first, last):
                for t in range(NT):
                    if t < NT - 2:
                        read_scores(h, a, t + 2, first)
                    elif not last:
                        read_scores(h + 1, 1 - a, t + 2 - NT, False)
                    dve.wait_ge(p_turned, 2 * (8 * h + t) + 1)
                    dve.tensor_copy(pT[t % 2][:, 0:8].rearrange("p c n -> p (c n)"), bank4[:].bitcast(I16)).then_inc(pT_lo, 1)
                    if t == 2 and not first:
                        finish_head(h - 1, 1 - a)
                if last:
                    finish_head(h, a)

            dve.wait_ge(q_step, 6 * NT)
            for t in range(2):
                read_scores(0, 0, t, True)
            sweep(dve, H, a1_head)

            dve.wait_ge(wp_loaded, 32)
            for t in range(NT):
                dve.wait_ge(o_proj, at(t))
                dve.tensor_tensor(xres[:, t], (bank6, bank7)[t % 2][:, :], xres[:, t], ALU.add).then_inc(o_added, 1)
                dve.wait_ge(o_added, 2 * t + 1)
                dve.tensor_tensor(xres[:, t], xres[:, t], bp_row, ALU.add).then_inc(o_added, 1)
            dve.wait_ge(o_added, 2 * NT)

            n = 0

            def f(ins):
                nonlocal n
                ins.then_inc(fw_step, 1)
                n += 1
                dve.wait_ge(fw_step, n)

            for w in range(3):
                dve.wait_ge(fw_loaded, 16 * (w + 1))
                f(dve.tensor_reduce(wsum, wld, X, ALU.add, apply_absolute_value=True))
                dve.tensor_reduce(wst[:, w:w + 1], wsum, X, ALU.add).then_inc(fw_sum, 1)
                dve.wait_ge(fw_all, w + 1)
                f(dve.tensor_scalar(wst[:, 6 + w:7 + w], wst[:, 3 + w:4 + w], 1.0 / (FI * D), 1e-5, ALU.mult, ALU.max))
                f(dve.reciprocal(wst[:, 9 + w:10 + w], wst[:, 6 + w:7 + w]))
                for j in range(2):
                    half = wld[:, j * FC // 2:(j + 1) * FC // 2]
                    f(dve.tensor_scalar(wtmp[:, 0], half, wst[:, 9 + w:10 + w], 0.5, ALU.mult, ALU.is_gt))
                    f(dve.tensor_scalar(wtmp[:, 1], half, wst[:, 9 + w:10 + w], -0.5, ALU.mult, ALU.is_lt))
                    if w and j == 0:
                        dve.wait_ge(fw_turned, FC * w)
                    dve.tensor_tensor(wint[:, j * FC // 2:(j + 1) * FC // 2], wtmp[:, 0], wtmp[:, 1], ALU.subtract).then_inc(fw_int, 1)
                    dve.wait_ge(fw_int, 2 * w + j + 1)

            layer_norm(3, xn4)
            dve.wait_ge(ln_step, 4 * LN_STEPS)
            n = 0

            def s(ins):
                nonlocal n
                ins.then_inc(f_step, 1)
                n += 1
                dve.wait_ge(f_step, n)

            s(dve.tensor_reduce(am4, xn4, X, ALU.max, apply_absolute_value=True))
            s(dve.tensor_scalar(sx4, am4, 1e-5, None, ALU.max))
            s(dve.reciprocal(sr4, sx4))
            s(dve.tensor_scalar(am4, sr4, 127.0, None, ALU.mult))
            s(dve.tensor_scalar(sr4, sx4, 1.0 / 127.0, None, ALU.mult))
            for w in range(2):
                s(dve.tensor_scalar(gscale[:, w], sr4, wst[:, 6 + w:7 + w], None, ALU.mult))
            for t in range(NT):
                dve.tensor_scalar(xn4[:, t], xn4[:, t], am4[:, t:t + 1], MAGIC, ALU.mult, ALU.add).then_inc(f_step, 1)
            n += NT
            for t in range(NT):
                dve.wait_ge(f_step, 7 + at(t))
                dve.tensor_scalar(xq4[:, t], xn4[:, t], MAGIC, None, ALU.subtract).then_inc(f_step, 1)
            n += NT
            assert n == F_STEPS_Q

            dve.wait_ge(fwT_ready, FW_GROUPS)
            dve.wait_ge(lnw_loaded, 16)
            hm = fsm[:, 6]

            def norm_hidden(t):
                dve.wait_ge(fsq_done, at(t))
                dve.tensor_tensor(hball[:, t], hball[:, t], lnw, ALU.mult).then_inc(fy_done, 1)
                dve.wait_ge(fy_done, 2 * t + 1)
                dve.tensor_reduce(hm[:, t:t + 1], hball[:, t], X, ALU.max, apply_absolute_value=True).then_inc(fy_done, 1)

            for t in range(NT):
                for q4 in range(4):
                    m = 4 * t + q4
                    dve.wait_ge(gu_done, 2 * m + 2)
                    dve.wait_ge(fsilu_done, at(m))
                    dve.scalar_tensor_tensor(hball[:, t, q4 * 512:(q4 + 1) * 512], (bank4, bank5)[q4 % 2][:, :], gscale[:, 1, t:t + 1],
                                             sgb[:, q4 * 512:(q4 + 1) * 512], ALU.mult, ALU.mult).then_inc(fh_done, 1)
                if t:
                    norm_hidden(t - 1)
            norm_hidden(NT - 1)
            dve.tensor_scalar(fsm[:, 0], ssq, 1.0 / FI, RMS_EPS, ALU.mult, ALU.add).then_inc(f_var, 1)
            dve.wait_ge(f_var, 1)
            n = 0
            n = rsqrt(fsm[:, 0], std0, fsm, (f_std, 1), f_step, F_STEPS_Q)
            dve.wait_ge(fy_done, 2 * NT)
            s(dve.tensor_tensor(fsm[:, 7], fsm[:, 1], hm, ALU.mult))
            s(dve.tensor_scalar(fsm[:, 8], fsm[:, 7], 1e-5, None, ALU.max))
            s(dve.reciprocal(fsm[:, 9], fsm[:, 8]))
            s(dve.scalar_tensor_tensor(fsm[:, 10], fsm[:, 9], 127.0, fsm[:, 1], ALU.mult, ALU.mult))
            s(dve.tensor_scalar(fsm[:, 11], fsm[:, 8], 1.0 / 127.0, wst[:, 8:9], ALU.mult, ALU.mult))

            def add_down(t):
                dve.wait_ge(fdown_done, at(t))
                dve.scalar_tensor_tensor(xres[:, t], (bank6, bank7)[t % 2][:, :], fsm[:, 11, t:t + 1], xres[:, t], ALU.mult, ALU.add).then_inc(fout_done, 1)

            for t in range(NT):
                dve.tensor_scalar(hball[:, t], hball[:, t], fsm[:, 10, t:t + 1], MAGIC, ALU.mult, ALU.add).then_inc(f2_step, 1)
                dve.wait_ge(f2_step, 2 * t + 1)
                if t:
                    dve.wait_ge(fh_turned, 2 * t)
                dve.tensor_scalar(hqr, hball[:, t], MAGIC, None, ALU.subtract).then_inc(f2_step, 1)
                if t:
                    add_down(t - 1)
            add_down(NT - 1)


_INS = ["x", "ctx_2048", "L0_ffn_gate_w", "L0_ffn_w1", "L0_ffn_w2", "L0_ffn_w3", "L1_xattn_Wq", "L1_xattn_bq", "L1_xattn_Wkv",
        "L1_xattn_bkv", "L1_xattn_Wp", "L1_xattn_bp", "L1_ffn_w_gate", "L1_ffn_w_up", "L1_ffn_w_down", "L1_ffn_ln_weight"]


def kernel(**inputs):
    import numpy as np
    import concourse.bacc as bacc
    from concourse.bass_utils import run_bass_kernel_spmd

    nc = bacc.Bacc("TRN2", target_bir_lowering=False, num_devices=1)
    arrays, args = {}, []
    for name in _INS:
        a = np.ascontiguousarray(inputs[name])
        arrays[f"in_{name}"] = a
        args.append(nc.dram_tensor(f"in_{name}", a.shape, mybir.dt.from_np(a.dtype), kind="ExternalInput").ap())
    args.append(nc.dram_tensor("out_0", (B, SQ, D), F32, kind="ExternalOutput").ap())
    program(nc, *args)
    return run_bass_kernel_spmd(nc, [arrays], core_ids=[0]).results[0]["out_0"]
```

```python
from contextlib import ExitStack

import concourse.bass as bass
from concourse import mybir

F32 = mybir.dt.float32
BF16 = mybir.dt.bfloat16
F16 = mybir.dt.float16
I16 = mybir.dt.int16
I32 = mybir.dt.int32
U8 = mybir.dt.uint8
ALU = mybir.AluOpType
ACT = mybir.ActivationFunctionType
X = mybir.AxisListType.X
BYTES = {F32: 4, I32: 4, BF16: 2, F16: 2, I16: 2, U8: 1}

P = 128
B, SQ, SK, D = 2, 512, 1024, 512
H, HD = 16, 32
T = B * SQ
NT = T // P
NC = B * SK // P
KC = D // P
E, EH = 8, 1024
EC = EH // P
SLOTS = 2 * T // P + E - 1
FI = 2048
FC = FI // P
UNITS = B * H
QT, KT = SQ // P, SK // P
HALF = KT - QT
WID = [SQ if k < HALF else SQ - P * (k - HALF) for k in range(KT)]
OFF = [sum(WID[:k]) for k in range(KT)]
NP = sum(WID)
KBLK, QBLK = 4, 5
KROW = KBLK * HD + 2
QROW = QBLK * HD
K3 = 3 * HD
K2 = 2 * HD
MAGIC = 12582912.0
LN255 = 5.541263545158426
MASKED = -1.0e30
SCALE = float(HD) ** -0.5
LN_EPS, RMS_EPS = 1e-5, 1e-6
CONSTS = 13
LN_STEPS = 3 * NT + 6
R_ASSIGNED, R_STEPS = 17, 36
F_SCALES = 7
F_STEPS_Q = F_SCALES + 2 * NT
FW_GROUPS = 3 * FC * KC // 8


def at(u):
    return u + 1


def xq_step(t):
    return min(2 * t + 3, 2 * NT)


def past(u, n):
    return not isinstance(u, int) or u >= n


def within(u, n):
    return not isinstance(u, int) or u < n


def sweep(eng, n, body):
    for u in range(2):
        body(u, u, 0, u == 0, u == n - 1)
    pairs = max((n - 3) // 2, 0)
    if pairs:
        with eng.Fori(1, pairs + 1) as i:
            body(2 * i, 0, i, False, False)
            body(2 * i + 1, 1, i, False, False)
    for u in range(2 + 2 * pairs, n):
        body(u, u % 2, u // 2, False, u == n - 1)


def turn_rows(pe, rows, ready, base, turned, copied, banks, ident):
    for t in range(NT):
        pe.wait_ge(ready, base + t + 1)
        if t >= 2:
            pe.wait_ge(copied, t - 1)
        for c in range(KC):
            ins = pe.transpose(banks[t % 2][:, c * P:(c + 1) * P], rows[:, t, c * P:(c + 1) * P], ident)
        ins.then_inc(turned, 1)


def program(nc, x, ctx_in, gate_w, w1, w2, w3, Wq, bq, Wkv, bkv, Wp, bp, w_gate, w_up, w_down, ln_w, out):
    with ExitStack() as stack:
        def sem(name):
            return stack.enter_context(nc.semaphore(name))

        ARENA = 207 * 1024
        arena = stack.enter_context(nc.sbuf_tensor("arena", [P, ARENA], U8))
        scores = stack.enter_context(nc.psum_tensor("scores", [P, 4 * 512], F32))
        bank4 = stack.enter_context(nc.psum_tensor("bank4", [P, 512], F32))
        bank5 = stack.enter_context(nc.psum_tensor("bank5", [P, 512], F32))
        bank6 = stack.enter_context(nc.psum_tensor("bank6", [P, 512], F32))
        bank7 = stack.enter_context(nc.psum_tensor("bank7", [P, 512], F32))

        class Region:

            def __init__(self, start, end=ARENA):
                self.at, self.end = start, end

            def take(self, dtype, *shape):
                n = BYTES[dtype]
                for s in shape:
                    n *= s
                view = arena[:, self.at:self.at + n].bitcast(dtype)
                self.at += (n + 31) // 32 * 32
                assert self.at <= self.end, "the region is full"
                names = "abcdef"[:len(shape)]
                if len(shape) > 1:
                    sizes = {names[i]: shape[i] for i in range(len(shape))}
                    view = view.rearrange(f"p ({' '.join(names)}) -> p {' '.join(names)}", **sizes)
                return view

        kst_d = nc.dram_tensor("kst_d", (H, K3, B * SK), BF16, kind="Internal").ap()
        qst_d = nc.dram_tensor("qst_d", (H, K3, T), BF16, kind="Internal").ap()
        xs_d = nc.dram_tensor("xs_d", (SLOTS * P, D), F32, kind="Internal").ap()
        tern_d = nc.dram_tensor("tern_d", (3, P, FI * D // P), BF16, kind="Internal").ap()
        v_d = nc.dram_tensor("v_d", (NC, P, D), F32, kind="Internal").ap()
        ys_d = nc.dram_tensor("ys_d", (SLOTS * P, D), F32, kind="Internal").ap()

        keep = Region(0)
        xres = keep.take(F32, NT, D)
        vint = keep.take(BF16, NC, D)
        svrow = keep.take(F32, D)
        idf = keep.take(F32, P)
        idb = keep.take(BF16, P)
        mask_q = keep.take(BF16, P)
        mask_k = keep.take(BF16, P)
        tri = keep.take(BF16, P)
        ones = keep.take(BF16, P)
        iota_e = keep.take(F32, E)
        iota_s = keep.take(F32, SLOTS + 1)
        stats = keep.take(F32, NT, 6)
        mv = keep.take(F32, NT, 2)
        std0 = keep.take(F32, NT)
        ln_t = keep.take(F32, 6, NT)
        wsums = keep.take(F32, NC, 3)
        wst = keep.take(F32, 5, 3)
        base = keep.at

        consts_made = sem("consts_made")
        x_loaded = [sem(f"x_loaded{b}") for b in range(B)]

        wkv_loaded = sem("wkv_loaded")
        ctx_loaded = [sem(f"ctx_loaded{a}") for a in range(2)]
        ctx_turned, ctxT_ready = sem("ctx_turned"), sem("ctxT_ready")
        c1_done, cr_done, c2_done, c3_done = (sem(n) for n in ("c1_done", "cr_done", "c2_done", "c3_done"))
        k_proj, v_proj, kf_done, vf_done = (sem(n) for n in ("k_proj", "v_proj", "kf_done", "vf_done"))
        k_step, kd_done = sem("k_step"), sem("kd_done")
        kq_done, kqr_done, krow_ready = (sem(n) for n in ("kq_done", "kqr_done", "krow_ready"))
        k_turned, kT_ready = sem("k_turned"), sem("kT_ready")
        kst_stored = [sem(f"kst_stored{a}") for a in range(2)]
        ones_set = sem("ones_set")
        v_step, vmax_ready, v_stored, v_back, v_made = (
            sem(n) for n in ("v_step", "vmax_ready", "v_stored", "v_back", "v_made"))

        rk = Region(base)
        kvrow = rk.take(BF16, B, H, KT, KROW)
        after_kvrow = rk.at
        wkv = rk.take(F32, KC, 2 * D)
        bkv_row = rk.take(F32, 2 * D)
        cin = [rk.take(F32, D) for _ in range(2)]
        cT = [rk.take(F32, KC, P) for _ in range(2)]
        cr = rk.take(F32, D)
        kf, kx, kr, kd, kqr = (rk.take(F32, H, HD) for _ in range(5))
        kam, ks, kinv = (rk.take(F32, H) for _ in range(3))
        krow = [rk.take(BF16, H, 3, HD) for _ in range(2)]
        kTbuf = [rk.take(BF16, H, P) for _ in range(2)]
        vf = rk.take(F32, NC, D)
        wpiece = [rk.take(F32, 3, D) for _ in range(2)]
        zero = rk.take(F32, D)
        vam = kf.rearrange("p a b -> p (a b)")

        ra = Region(after_kvrow)
        qrow = ra.take(BF16, B, H, QT, QROW)
        kst = [ra.take(BF16, KT, KROW) for _ in range(2)]
        vst = [ra.take(BF16, KT, KROW) for _ in range(2)]
        qst = [ra.take(BF16, QT, QROW) for _ in range(2)]
        kA = [ra.take(BF16, SK) for _ in range(2)]
        kC = [ra.take(BF16, SK) for _ in range(2)]
        qA = [ra.take(BF16, SQ) for _ in range(2)]
        qC = [ra.take(BF16, SQ) for _ in range(2)]
        oatt = ra.take(F32, B, H, QT, HD)
        xn0 = oatt.rearrange("p b h t d -> p (b h t d)").rearrange("p (t d) -> p t d", t=NT)
        qr = Region(ra.at).take(F32, NT, D)
        eP = ra.take(F32, NP)
        p1 = ra.take(F16, NP)
        p2 = ra.take(F16, NP)
        mx = ra.take(F32, QT)
        mparts = ra.take(BF16, QT, 2)
        osum = ra.take(F32, QT, HD)
        rl = ra.take(F32, QT)

        rm = Region(base)
        wbuf = [(rm.take(F32, 2, KC, EH), rm.take(F32, EC, D)) for _ in range(2)]
        xsin = [rm.take(F32, D) for _ in range(2)]
        xsT = [rm.take(F32, KC, P) for _ in range(2)]
        sg = rm.take(F32, EH)
        hb = rm.take(F32, EH)
        hT = rm.take(F32, EC, P)
        yb = [rm.take(F32, D) for _ in range(2)]
        posi = rm.take(I32, 2, NT)
        slot_e = rm.take(I32, SLOTS + 1)
        r1 = [rm.take(F32, NT) for _ in range(10)]
        vinv = rm.take(F32, D)
        m_mark = rm.at
        xn = rm.take(F32, NT, D)
        XT = rm.take(F32, KC, T)
        gw = rm.take(F32, D)
        gwT = rm.take(F32, KC, E)
        r8 = [rm.take(F32, NT, E) for _ in range(12)]
        asg = rm.take(BF16, NT, E)
        te = [rm.take(F32, E) for _ in range(6)]
        cmp = rm.take(F32, SLOTS + 1, E)
        slot_f = rm.take(F32, SLOTS + 1)
        rw = Region(m_mark)
        WCOLS = 4 * D
        wchunk = [rw.take(F32, WCOLS) for _ in range(2)]
        above, below = (rw.take(BF16, WCOLS) for _ in range(2))
        tern = [rw.take(BF16, WCOLS) for _ in range(2)]
        vchunk = [wchunk[a].rearrange("p (t d) -> p t d", d=D) for a in range(2)]
        gath = Region(base)
        grow = [gath.take(F32, D) for _ in range(2 * NT)]

        rq = Region(base)
        xn3 = rq.take(F32, NT, D)
        XT3 = rq.take(F32, KC, T)
        wq_sb = rq.take(F32, KC, D)
        bq_row = rq.take(F32, D)
        wp_sb = rq.take(F32, KC, D)
        bp_row = rq.take(F32, D)
        qf, qx = (rq.take(F32, H, HD) for _ in range(2))
        qam, qsv, qinv = (rq.take(F32, H) for _ in range(3))
        nsq = rq.take(F32, H, NT)
        q3row = [rq.take(BF16, H, 3, HD) for _ in range(2)]
        qTbuf = [rq.take(BF16, H, P) for _ in range(2)]
        khead = [rq.take(BF16, B * SK) for _ in range(2)]
        qhead = [rq.take(BF16, T) for _ in range(2)]
        vhead = [rq.take(BF16, NC, HD) for _ in range(2)]
        ssb = [rq.take(F32, B * SK) for _ in range(2)]
        nmx = [rq.take(F32, 2) for _ in range(2)]
        ebias = [rq.take(F32, 1) for _ in range(2)]
        p16 = [rq.take(I16, B * SK) for _ in range(2)]
        pT = [rq.take(BF16, NC, P) for _ in range(2)]
        rsum = [rq.take(F32, NT) for _ in range(2)]
        rrec = rq.take(F32, NT)
        otmp = rq.take(F32, NT, HD)
        oh = rq.take(F32, NT, D)
        frow = [rq.take(BF16, FC, D) for _ in range(2)]

        rf = Region(base)
        xn4 = rf.take(F32, NT, D)
        xq4 = rf.take(BF16, NT, D)
        xT4 = rf.take(BF16, KC, T)
        wT = [rf.take(BF16, KC, FI) for _ in range(2)]
        wdT = rf.take(BF16, FC, D)
        lnw = rf.take(F32, FI)
        am4, sx4, sr4 = (rf.take(F32, NT) for _ in range(3))
        gscale = rf.take(F32, 2, NT)
        ssq = rf.take(F32, NT)
        fsm = rf.take(F32, 12, NT)
        f_mark = rf.at
        frow.append(rf.take(BF16, FC, D))
        rg = Region(f_mark)
        hball = rg.take(F32, NT, FI)
        sgb = rg.take(F32, FI)
        hqr = [rg.take(BF16, FI), sgb.bitcast(BF16)[:, 0:FI]]
        hqT = [rg.take(BF16, FC, P), sgb.bitcast(BF16)[:, FI:2 * FI].rearrange("p (c n) -> p c n", n=P)]

        def context_parts(u):
            rows = kvrow.rearrange("p b h t c -> p b h (t c)")
            view = rows[:, bass.ds(u // KT, 1), :, bass.ds((u % KT) * KROW, KBLK * HD)]
            return view.rearrange("p b h (c d) -> p (b h) c d", d=HD)

        w_rows = [w_gate, w_up, w_down.rearrange("o (c n) -> (o c) n", n=D)]

        def by_head(row):
            return row.rearrange("p (h d) -> p h d", h=H)

        def each(col, shape):
            return col.rearrange("p (n o) -> p n o", o=1).broadcast_to([P] + shape)

        x_t = x.rearrange("b (t p) d -> p (b t) d", p=P)
        out_t = out.rearrange("b (t p) d -> p (b t) d", p=P)
        ctx_t = ctx_in.rearrange("b (t p) d -> (b t) p d", p=P)

        ln_step, ln_var, ln_std = sem("ln_step"), sem("ln_var"), sem("ln_std")
        qs12, qs_r, qs3 = (sem(n) for n in ("qs12", "qs_r", "qs3"))
        qrow_ready = sem("qrow_ready")
        k_staged, v_in, q_staged = ([sem(f"{n}{a}") for a in range(2)] for n in ("k_staged", "v_in", "q_staged"))
        k0_turned, q_turned, m_turned = (sem(n) for n in ("k0_turned", "q_turned", "m_turned"))
        ka_ready, kc_ready, q_ready, m_ready = (sem(n) for n in ("ka_ready", "kc_ready", "q_ready", "m_ready"))
        smax_done, max_done, m_step = sem("smax_done"), sem("max_done"), sem("m_step")
        st_done, exp_done, p1_done, p2_done = (sem(n) for n in ("st_done", "exp_done", "p1_done", "p2_done"))
        pv_done, oread_done, o_done = (sem(n) for n in ("pv_done", "oread_done", "o_done"))
        att_added = sem("att_added")
        gw_loaded, xs_zeroed = sem("gw_loaded"), sem("xs_zeroed")
        zero_made = sem("zero_made")
        gw_turned, gwT_ready = sem("gw_turned"), sem("gwT_ready")
        xn_turned, xT_ready, logits_done = sem("xn_turned"), sem("xT_ready"), sem("logits_done")
        r_step, r_exp, ranks_done = sem("r_step"), sem("r_exp"), sem("ranks_done")
        scattered = sem("scattered")
        gathered = [sem(f"gathered{t}") for t in range(NT // 2)]
        w13_loaded = [sem(f"w13_loaded{a}") for a in range(2)]
        w2_loaded = [sem(f"w2_loaded{a}") for a in range(2)]
        xs_loaded = [sem(f"xs_loaded{a}") for a in range(2)]
        xs_turned, xsT_ready = sem("xs_turned"), sem("xsT_ready")
        up_done, silu_done, h_done = sem("up_done"), sem("silu_done"), sem("h_done")
        h_turned, hT0_ready, hT1_ready = sem("h_turned"), sem("hT0_ready"), sem("hT1_ready")
        y_done, y_ready = sem("y_done"), sem("y_ready")
        y_stored = [sem(f"y_stored{a}") for a in range(2)]
        moe_added = sem("moe_added")
        wq_loaded, wp_loaded = sem("wq_loaded"), sem("wp_loaded")
        x3_turned, x3T_ready = sem("x3_turned"), sem("x3T_ready")
        q_proj, qf_done, q_step, q3_ready = (sem(n) for n in ("q_proj", "qf_done", "q_step", "q3_ready"))
        q3_turned, qT_ready = sem("q3_turned"), sem("qT_ready")
        qst_stored = [sem(f"qst_stored{a}") for a in range(2)]
        k_loaded = [sem(f"k_loaded{a}") for a in range(2)]
        v_staged = sem("v_staged")
        s_done, s_read, bias_ready = sem("s_done"), sem("s_read"), sem("bias_ready")
        p_ready, p_turned, pT_lo, pT_hi = (sem(n) for n in ("p_ready", "p_turned", "pT_lo", "pT_hi"))
        av_done, a_post = sem("av_done"), sem("a_post")
        o_turned, oT_ready, o_proj, o_added = (sem(n) for n in ("o_turned", "oT_ready", "o_proj", "o_added"))
        wpiece_loaded = [sem(f"wpiece_loaded{a}") for a in range(2)]
        wpiece_done, wsum_done, wsum_all, w_mean = (sem(n) for n in ("wpiece_done", "wsum_done", "wsum_all", "w_mean"))
        w_in = [sem(f"w_in{a}") for a in range(2)]
        w_step, tern_made = sem("w_step"), sem("tern_made")
        tern_stored = [sem(f"tern_stored{a}") for a in range(2)]
        frow_loaded, fd_loaded, lnw_loaded = sem("frow_loaded"), sem("fd_loaded"), sem("lnw_loaded")
        fw_turned, fwT_ready = sem("fw_turned"), sem("fwT_ready")
        f_step, x4_turned, x4T_ready = sem("f_step"), sem("x4_turned"), sem("x4T_ready")
        gu_done, fsilu_done, fh_done, fsq_done, fy_done, fmax_done = (
            sem(n) for n in ("gu_done", "fsilu_done", "fh_done", "fsq_done", "fy_done", "fmax_done"))
        f2_step, fh_turned, fhT_ready, fdown_done, fout_done = (
            sem(n) for n in ("f2_step", "fh_turned", "fhT_ready", "fdown_done", "fout_done"))
        stored = sem("stored")

        block = stack.enter_context(nc.Block())

        @block.sync
        def _(sp):
            def store_v(u):
                sp.wait_ge(vf_done, at(u))
                sp.dma_start(v_d[bass.ds(u, 1)].rearrange("t p d -> p (t d)"), vf[:, bass.ds(u, 1)].rearrange("p u d -> p (u d)")).then_inc(v_stored, 16)

            def load_ctx(u, a, k, first, last):
                if past(u, 2):
                    sp.wait_ge(ctx_turned, at(u - 2))
                    sp.wait_ge(c1_done, at(u - 2))
                    sp.wait_ge(cr_done, at(u - 2))
                sp.dma_start(cin[a], ctx_t[bass.ds(u, 1)].rearrange("a p d -> p (a d)")).then_inc(ctx_loaded[a], 16)
                if past(u, 2):
                    sp.wait_ge(wpiece_done, at(u - 2))
                for w in range(3):
                    sp.dma_start(wpiece[a][:, w], w_rows[w][bass.ds(u * P, P), :]).then_inc(wpiece_loaded[a], 16)
                if past(u, 2):
                    store_v(u - 2)

            sweep(sp, NC, load_ctx)
            for b in range(B):
                sp.dma_start(xres[:, b * QT:(b + 1) * QT, :], x_t[:, b * QT:(b + 1) * QT, :]).then_inc(x_loaded[b], 16)
            for u in (NC - 2, NC - 1):
                store_v(u)
            sp.wait_ge(zero_made, 1)
            for s in range(SLOTS):
                sp.dma_start(xs_d[s * P:(s + 1) * P, :], zero).then_inc(xs_zeroed, 16)

            sp.wait_ge(qrow_ready, 1)
            k_rows = kvrow.rearrange("p b h t c -> p (b h) (t c)")
            q_rows = qrow.rearrange("p b h t c -> p (b h) (t c)")

            def stage_unit(u, a, k, first, last):
                if past(u, 2):
                    sp.wait_ge(k0_turned, at(u - 2))
                    sp.wait_ge(q_turned, at(u - 2))
                sp.dma_start(kst[a].rearrange("p t c -> p (t c)"), k_rows[:, bass.ds(u, 1)].rearrange("p u c -> p (u c)")).then_inc(k_staged[a], 16)
                sp.dma_start(qst[a].rearrange("p t c -> p (t c)"), q_rows[:, bass.ds(u, 1)].rearrange("p u c -> p (u c)")).then_inc(q_staged[a], 16)
                if past(u, 2):
                    sp.wait_ge(pv_done, 4 * (u - 1))
                sp.dma_start(vst[a].rearrange("p t c -> p (t c)"), k_rows[:, bass.ds(u, 1)].rearrange("p u c -> p (u c)")).then_inc(v_in[a], 16)

            sweep(sp, UNITS, stage_unit)

            sp.wait_ge(att_added, NT)
            sp.dma_start(gw[0:E, :], gate_w).then_inc(gw_loaded, 16)

            sp.wait_ge(r_step, R_STEPS)
            with sp.register("expert") as expert:
                def load_slot(u, a, k, first, last):
                    sp.reg_load(expert, slot_e[0:1, bass.ds(u, 1)])
                    e = sp.snap(expert)
                    if past(u, 2):
                        sp.wait_ge(xs_turned, at(u - 2))
                    if not first:
                        sp.dma_start(xsin[a], xs_d[bass.ds(u * P, P), :]).then_inc(xs_loaded[a], 16)
                    if past(u, 2):
                        sp.wait_ge(up_done, 4 * (u - 1))
                    sp.dma_start(wbuf[a][0][:, 0], w1[bass.ds(e, 1)].rearrange("e (k p) n -> p (e k) n", p=P)).then_inc(w13_loaded[a], 16)
                    sp.dma_start(wbuf[a][0][:, 1], w3[bass.ds(e, 1)].rearrange("e (k p) n -> p (e k) n", p=P)).then_inc(w13_loaded[a], 16)
                    if first:
                        sp.wait_ge(scattered, 16 * 2 * NT)
                        sp.dma_start(xsin[a], xs_d[bass.ds(u * P, P), :]).then_inc(xs_loaded[a], 16)
                    if past(u, 2):
                        sp.wait_ge(y_done, at(u - 2))
                    sp.dma_start(wbuf[a][1], w2[bass.ds(e, 1)].rearrange("e (k p) n -> p (e k) n", p=P)).then_inc(w2_loaded[a], 16)

                sweep(sp, SLOTS, load_slot)

            sp.wait_ge(moe_added, 2 * NT)
            sp.dma_start(wq_sb, Wq.rearrange("(k p) n -> p k n", p=P)).then_inc(wq_loaded, 16)
            sp.dma_start(bq_row, bq.partition_broadcast(P)).then_inc(wq_loaded, 16)
            for a in range(2):
                sp.wait_ge(tern_stored[a], 16 * 6)
            for w in range(2):
                sp.dma_start(frow[w].rearrange("p o n -> p (o n)"), tern_d[w]).then_inc(frow_loaded, 16)
            sp.dma_start(wp_sb, Wp.rearrange("(k p) n -> p k n", p=P)).then_inc(wp_loaded, 16)
            sp.dma_start(bp_row, bp.partition_broadcast(P)).then_inc(wp_loaded, 16)

            for a in range(2):
                sp.wait_ge(qst_stored[a], 16 * (NT // 2))
                sp.wait_ge(kst_stored[a], 16 * (NC // 2))

            def load_head(u, a, k, first, last):
                if past(u, 2):
                    sp.wait_ge(s_done, 16 * (u - 1))
                sp.dma_start(khead[a][0:K3, :], kst_d[bass.ds(u, 1)].rearrange("h r n -> r (h n)")).then_inc(k_loaded[a], 16)
                sp.dma_start(qhead[a][0:K3, :], qst_d[bass.ds(u, 1)].rearrange("h r n -> r (h n)")).then_inc(k_loaded[a], 16)

            sweep(sp, H, load_head)

            sp.wait_ge(o_added, 2 * NT)
            sp.dma_start(frow[2].rearrange("p o n -> p (o n)"), tern_d[2]).then_inc(fd_loaded, 16)
            sp.dma_start(lnw, ln_w.partition_broadcast(P)).then_inc(lnw_loaded, 16)

            for t in range(NT):
                sp.wait_ge(fout_done, at(t))
                sp.dma_start(out_t[:, t, :], xres[:, t, :]).then_inc(stored, 16)
            sp.wait_ge(stored, 16 * NT)

        @block.gpsimd
        def _(pool):
            n = 0

            def made(ins):
                nonlocal n
                ins.then_inc(consts_made, 1)
                n += 1
                pool.wait_ge(consts_made, n)

            for m, fill in ((idf, 0.0), (idb, 0.0), (mask_q, 0.0), (mask_k, 0.0), (tri, 1.0), (ones, 1.0)):
                made(pool.memset(m, fill))
            for m in (idf, idb):
                made(pool.affine_select(out=m, in_=m, compare_op=ALU.not_equal, fill=1.0, base=0,
                                        pattern=[[-1, P]], channel_multiplier=1))
            made(pool.affine_select(out=mask_q, in_=mask_q, compare_op=ALU.is_ge, fill=MASKED, base=0,
                                    pattern=[[-1, P]], channel_multiplier=1))
            made(pool.affine_select(out=mask_k, in_=mask_k, compare_op=ALU.is_ge, fill=MASKED, base=0,
                                    pattern=[[1, P]], channel_multiplier=-1))
            made(pool.affine_select(out=tri, in_=tri, compare_op=ALU.is_gt, fill=0.0, base=0,
                                    pattern=[[1, P]], channel_multiplier=-1))
            made(pool.iota(iota_e, pattern=[[1, E]], base=0, channel_multiplier=0, allow_small_or_imprecise_dtypes=True))
            made(pool.iota(iota_s, pattern=[[1, SLOTS + 1]], base=0, channel_multiplier=0, allow_small_or_imprecise_dtypes=True))
            assert n == CONSTS
            pool.memset(zero, 0.0).then_inc(zero_made, 1)
            pool.memset(kvrow[:, :, :, :, KBLK * HD:KROW].rearrange("p b h t c -> p (b h t) c"), 1.0).then_inc(ones_set, 1)

            def store_k(u, a, k, first, last):
                pool.wait_ge(kT_ready, 2 * u + 2)
                pool.dma_start(kst_d[:, :, bass.ds(u * P, P)].rearrange("h r n -> r h n"), kTbuf[a][0:K3]).then_inc(kst_stored[a], 16)


            sweep(pool, NC, store_k)
            pool.wait_ge(v_step, 1)
            pool.partition_all_reduce(svrow, vam, P, bass.bass_isa.ReduceOp.absmax).then_inc(vmax_ready, 1)
            pool.wait_ge(vmax_ready, 1)
            pool.wait_ge(wsum_done, 1)
            pool.partition_all_reduce(wst[:, 1], wst[:, 0], P, bass.bass_isa.ReduceOp.add).then_inc(wsum_all, 1)
            pool.wait_ge(wsum_all, 1)

            pool.wait_ge(qrow_ready, 1)
            for a in range(2):
                pool.memset(kC[a][K2:K2 + 2, :], 1.0).then_inc(ones_set, 1)

            pool.wait_ge(r_step, R_STEPS)
            pool.wait_ge(xs_zeroed, 16 * SLOTS)
            for t in range(NT):
                for j in range(2):
                    pool.indirect_dma_start(xs_d, bass.IndirectOffsetOnAxis(ap=posi[:, j, t:t + 1], axis=0), xn[:, t, :], None).then_inc(scattered, 16)

            pool.wait_ge(scattered, 16 * 2 * NT)
            pool.wait_ge(v_step, 3)
            for g in range(NC // 4):
                a, tiles = g % 2, slice(4 * g, 4 * g + 4)
                if g >= 2:
                    pool.wait_ge(v_made, 3 * (g - 1))
                pool.dma_start(vchunk[a], v_d[tiles].rearrange("t p d -> p t d")).then_inc(v_back, 16)
                pool.wait_ge(v_back, 16 * (g + 1))
                pool.tensor_tensor(vchunk[a], vchunk[a], vinv.rearrange("p (o d) -> p o d", o=1).broadcast_to([P, 4, D]), ALU.mult).then_inc(v_made, 1)
                pool.wait_ge(v_made, 3 * g + 1)
                pool.tensor_scalar(vchunk[a], vchunk[a], MAGIC, None, ALU.add).then_inc(v_made, 1)
                pool.wait_ge(v_made, 3 * g + 2)
                pool.tensor_scalar(vint[:, tiles], vchunk[a], MAGIC, None, ALU.subtract).then_inc(v_made, 1)

            pool.wait_ge(scattered, 16 * 2 * NT)
            pool.wait_ge(w_mean, 3)

            def load_chunk(g):
                w, c, a = g // 4, g % 4, g % 2
                if w < 2:
                    src = w_rows[w].rearrange("(o p) n -> p o n", p=P)[:, 4 * c:4 * c + 4]
                    pool.dma_start(wchunk[a].rearrange("p (o n) -> p o n", n=D), src).then_inc(w_in[a], 16)
                else:
                    pool.dma_start(wchunk[a], w_down[c * P:(c + 1) * P, :]).then_inc(w_in[a], 16)

            def f(ins):
                ins.then_inc(w_step, 1)

            pool.wait_ge(v_made, 3 * NC // 4)
            load_chunk(0)
            for g in range(12):
                w, c, a = g // 4, g % 4, g % 2
                if g < 11:
                    if g:
                        pool.wait_ge(w_step, 2 * g)
                    load_chunk(g + 1)
                if g:
                    pool.wait_ge(tern_made, g)
                if g >= 2:
                    pool.wait_ge(tern_stored[a], 16 * (g // 2))
                pool.wait_ge(w_in[a], 16 * (g // 2 + 1))
                f(pool.tensor_scalar(above, wchunk[a], wst[:, 3, w:w + 1], None, ALU.is_gt))
                f(pool.tensor_scalar(below, wchunk[a], wst[:, 4, w:w + 1], None, ALU.is_lt))
                pool.wait_ge(w_step, 2 * g + 2)
                pool.tensor_tensor(tern[a], above, below, ALU.subtract).then_inc(tern_made, 1)
                pool.wait_ge(tern_made, g + 1)
                pool.dma_start(tern_d[w][:, c * WCOLS:(c + 1) * WCOLS], tern[a]).then_inc(tern_stored[a], 16)

            for a, m in ((0, (SLOTS + 1) // 2), (1, SLOTS // 2)):
                pool.wait_ge(y_stored[a], 16 * m)
            for t in range(NT):
                for j in range(2):
                    pool.indirect_dma_start(grow[2 * t + j], None, ys_d, bass.IndirectOffsetOnAxis(ap=posi[:, j, t:t + 1], axis=0)).then_inc(gathered[t // 2], 16)

            def store_q(u, a, k, first, last):
                pool.wait_ge(qT_ready, 2 * u + 2)
                pool.dma_start(qst_d[:, :, bass.ds(u * P, P)].rearrange("h r n -> r h n"), qTbuf[a][0:K3]).then_inc(qst_stored[a], 16)

            sweep(pool, NT, store_q)

            def stage_v(u, a, k, first, last):
                if past(u, 2):
                    pool.wait_ge(av_done, 8 * (u - 1))
                pool.tensor_copy(vhead[a], vint[:, :, bass.ds(u * HD, HD)]).then_inc(v_staged, 1)

            pool.wait_ge(moe_added, 2 * NT)
            pool.wait_ge(v_made, 3 * NC // 4)
            sweep(pool, H, stage_v)

            pool.wait_ge(lnw_loaded, 16)
            for t in range(NT):
                pool.wait_ge(fsq_done, at(t))
                pool.tensor_tensor(hball[:, t], hball[:, t], lnw, ALU.mult).then_inc(fy_done, 1)

        @block.tensor
        def _(pe):
            pe.wait_ge(consts_made, CONSTS)

            def turn_k(u, a):
                pe.wait_ge(krow_ready, at(u))
                if past(u, 1):
                    pe.wait_ge(kT_ready, 2 * u)
                for g, bank in enumerate((bank4, bank5)):
                    view = bank[:].bitcast(BF16)
                    for h in range(8):
                        ins = pe.transpose(view[0:K3, h * P:(h + 1) * P],
                                           krow[a][:, 8 * g + h].rearrange("p c d -> p (c d)"), idb)
                    ins.then_inc(k_turned, 1)

            def turn_ctx(u, a, k):
                pe.wait_ge(ctx_loaded[a], 16 * (k + 1))
                if past(u, 1):
                    pe.wait_ge(ctxT_ready, at(u - 1))
                for c in range(KC):
                    ins = pe.transpose(bank6[:, c * P:(c + 1) * P], cin[a][:, c * P:(c + 1) * P], idf)
                ins.then_inc(ctx_turned, 1)

            def kv_tile(u, a, k, first, last):
                if first:
                    turn_ctx(0, 0, 0)
                if not last:
                    turn_ctx(u + 1, 1 - a, k + a)
                pe.wait_ge(ctxT_ready, at(u))
                if first:
                    pe.wait_ge(wkv_loaded, 32)
                else:
                    pe.wait_ge(kf_done, at(u - 1))
                for c in range(KC):
                    ins = pe.matmul(scores[:, 0:D], cT[a][:, c], wkv[:, c, 0:D], start=c == 0, stop=c == KC - 1)
                ins.then_inc(k_proj, 1)
                if not first:
                    pe.wait_ge(vf_done, at(u - 1))
                for c in range(KC):
                    ins = pe.matmul(scores[:, D:2 * D], cT[a][:, c], wkv[:, c, D:2 * D], start=c == 0, stop=c == KC - 1)
                ins.then_inc(v_proj, 1)
                if not first:
                    turn_k(u - 1, 1 - a)
                if last:
                    turn_k(u, a)

            sweep(pe, NC, kv_tile)

            def turn_keys(u, a, k):
                pe.wait_ge(k_staged[a], 16 * (k + 1))
                if past(u, 1):
                    pe.wait_ge(q_ready, 2 * u)
                else:
                    pe.wait_ge(ctxT_ready, at(NC - 1))
                view = bank6[:].bitcast(BF16)
                for t in range(KT):
                    ins = pe.transpose(view[:, t * P:(t + 1) * P], kst[a][:, t, 0:P], idb)
                ins.then_inc(k0_turned, 1)

            def turn_queries(u, a, k):
                pe.wait_ge(q_staged[a], 16 * (k + 1))
                pe.wait_ge(ka_ready, at(u))
                view = bank6[:].bitcast(BF16)
                for t in range(QT):
                    pe.transpose(view[:, t * P:(t + 1) * P], qst[a][:, t, HD:HD + P], idb)
                for t in range(QT):
                    ins = pe.transpose(view[0:K2, SQ + t * P:SQ + (t + 1) * P], qst[a][:, t, 0:K2], idb)
                ins.then_inc(q_turned, 1)

            def smax(u, b, t):
                s = 1024 * (t % 2)
                if t == 0:
                    pe.wait_ge(q_ready, 2 * u + 1)
                    if past(u, 1):
                        pe.wait_ge(m_ready, at(u - 1))
                if past(u, 1) or t >= 2:
                    pe.wait_ge(max_done, QT * u + t - 1)
                q = qA[b][:, t * P:(t + 1) * P]
                pe.matmul(scores[:, s:s + 512], q, kA[b][:, 0:512], start=True, stop=True)
                n = (t + 1) * P
                pe.matmul(scores[:, s + 512:s + 512 + n], q, kA[b][:, 512:512 + n], start=True, stop=False)
                pe.matmul(scores[:, s + 512 + n - P:s + 512 + n], idb, mask_q, start=False, stop=True).then_inc(smax_done, 1)

            def turn_m(u, b):
                pe.wait_ge(m_step, 2 * u + 2)
                view = scores[:, 0:512].bitcast(BF16)
                for t in range(QT):
                    ins = pe.transpose(view[K2:K2 + 2, t * P:(t + 1) * P], mparts[:, t, 0:2], idb)
                ins.then_inc(m_turned, 1)

            def st(u, a, k, first):
                if k == 0:
                    pe.wait_ge(kc_ready, at(u))
                    pe.wait_ge(m_ready, at(u))
                if not (first and k < 2):
                    pe.wait_ge(exp_done, KT * u + k - 1)
                else:
                    pe.wait_ge(kT_ready, 2 * NC)
                bank = (bank4, bank5)[k % 2]
                w = WID[k]
                diag = k >= HALF
                pe.matmul(bank[:, 0:w], kA[a][:, k * P:(k + 1) * P], qA[a][:, SQ - w:SQ], start=True, stop=False)
                ins = pe.matmul(bank[:, 0:w], kC[a][0:K2 + 2, k * P:(k + 1) * P], qC[a][0:K2 + 2, SQ - w:SQ], start=False, stop=not diag)
                if diag:
                    ins = pe.matmul(bank[:, 0:P], idb, mask_k, start=False, stop=True)
                ins.then_inc(st_done, 1)

            def pv(u, a, k, r, first):
                if k == 0:
                    pe.wait_ge(v_in[a], 16 * (r + 1))
                    if not first:
                        pe.wait_ge(oread_done, 2 * u)
                if k % 2 == 0:
                    pe.wait_ge(p2_done, 4 * u + k // 2 + 1)
                    pe.wait_ge(p1_done, 4 * u + k // 2 + 1)
                for t in range(max(0, k - HALF), QT):
                    c = OFF[k] + (t * P - (SQ - WID[k]))
                    for part in (p1, p2):
                        ins = pe.matmul(bank7[:, t * 97:t * 97 + 97], part[:, c:c + P], vst[a][:, k, HD:HD + 97],
                                        start=(k == 0 and t == 0 and part is p1), stop=(k == KT - 1 and t == QT - 1 and part is p2),
                                        skip_group_check=True)
                if k % 2:
                    ins.then_inc(pv_done, 1)

            def att_unit(u, a, r, first, last):
                b = 1 - a
                if not last:
                    smax(u + 1, b, 0); smax(u + 1, b, 1)
                st(u, a, 2, first); st(u, a, 3, first)
                if not last:
                    smax(u + 1, b, 2)
                st(u, a, 4, first); st(u, a, 5, first)
                pv(u, a, 0, r, first); pv(u, a, 1, r, first)
                if not last:
                    smax(u + 1, b, 3)
                st(u, a, 6, first); st(u, a, 7, first)
                if within(u + 2, UNITS):
                    turn_keys(u + 2, a, r + 1)
                pv(u, a, 2, r, first); pv(u, a, 3, r, first)
                if not last:
                    turn_m(u + 1, b)
                if within(u + 2, UNITS):
                    turn_queries(u + 2, a, r + 1)
                if not last:
                    st(u + 1, b, 0, False); st(u + 1, b, 1, False)
                pv(u, a, 4, r, first); pv(u, a, 5, r, first)
                pv(u, a, 6, r, first); pv(u, a, 7, r, first)

            turn_keys(0, 0, 0)
            turn_queries(0, 0, 0)
            pe.wait_ge(vf_done, NC)
            pe.wait_ge(ones_set, 3)
            for t in range(QT):
                smax(0, 0, t)
            turn_m(0, 0)
            turn_keys(1, 1, 0)
            turn_queries(1, 1, 0)
            st(0, 0, 0, True); st(0, 0, 1, True)
            sweep(pe, UNITS, att_unit)

            pe.wait_ge(gw_loaded, 16)
            pe.wait_ge(m_ready, UNITS)
            pe.wait_ge(exp_done, UNITS * KT)
            pe.wait_ge(oread_done, 2 * UNITS)
            for c in range(KC):
                ins = pe.transpose(bank6[:, c * E:(c + 1) * E], gw[0:E, c * P:(c + 1) * P], idf[0:E, 0:E])
            ins.then_inc(gw_turned, 1)
            turn_rows(pe, xn, ln_step, LN_STEPS * 2 - NT, xn_turned, xT_ready, (bank4, bank5), idf)
            pe.wait_ge(gwT_ready, 1)
            pe.wait_ge(xT_ready, NT)
            for t in range(NT):
                for c in range(KC):
                    ins = pe.matmul(bank7[:, t * E:(t + 1) * E], XT[:, c, t * P:(t + 1) * P], gwT[:, c], start=c == 0, stop=c == KC - 1)
            ins.then_inc(logits_done, 1)
            pe.wait_ge(r_step, R_ASSIGNED)
            pe.wait_ge(gwT_ready, 1)
            flat = asg.rearrange("p t e -> p (t e)")
            pe.matmul(bank6[:, 0:NT * E], tri, flat, start=True, stop=False, skip_group_check=True)
            for s in range(1, NT):
                pe.matmul(bank6[:, s * E:NT * E], ones, flat[:, 0:(NT - s) * E], start=False, stop=s == NT - 1, skip_group_check=True)
            for t in range(NT):
                ins = pe.matmul(bank7[:, 128:128 + E], ones, asg[:, t], start=t == 0, stop=t == NT - 1)
            ins.then_inc(ranks_done, 1)

            def turn_slot(u, a, k):
                pe.wait_ge(xs_loaded[a], 16 * (k + 1))
                for c in range(KC):
                    ins = pe.transpose(bank6[:, c * P:(c + 1) * P], xsin[a][:, c * P:(c + 1) * P], idf)
                ins.then_inc(xs_turned, 1)

            def slot(u, a, k, first, last):
                wa, wb = wbuf[a]
                if first:
                    turn_slot(0, 0, 0)
                pe.wait_ge(xsT_ready, at(u))
                pe.wait_ge(w13_loaded[a], 32 * (k + 1))
                for half in range(2):
                    if not first:
                        pe.wait_ge(h_done, 2 * (u - 1) + half + 1)
                    for m in range(2):
                        for c in range(KC):
                            ins = pe.matmul(scores[:, m * 1024 + half * 512:m * 1024 + half * 512 + 512], xsT[a][:, c],
                                            wa[:, m, c, half * 512:half * 512 + 512], start=c == 0, stop=c == KC - 1)
                        ins.then_inc(up_done, 1)
                if not last:
                    turn_slot(u + 1, 1 - a, k + a)
                for half, bank in enumerate((bank4, bank5)):
                    pe.wait_ge(h_done, 2 * u + half + 1)
                    for c in range(4):
                        ins = pe.transpose(bank[:, c * P:(c + 1) * P], hb[:, (4 * half + c) * P:(4 * half + c + 1) * P], idf)
                    ins.then_inc(h_turned, 1)
                pe.wait_ge(w2_loaded[a], 16 * (k + 1))
                for half, ready in enumerate((hT0_ready, hT1_ready)):
                    pe.wait_ge(ready, at(u))
                    if half == 0 and not first:
                        pe.wait_ge(y_ready, at(u - 1))
                    for c in range(4 * half, 4 * half + 4):
                        ins = pe.matmul(bank7[:, :], hT[:, c], wb[:, c], start=c == 0, stop=c == EC - 1)
                ins.then_inc(y_done, 1)

            sweep(pe, SLOTS, slot)

            pe.wait_ge(hT0_ready, SLOTS)
            pe.wait_ge(hT1_ready, SLOTS)
            pe.wait_ge(y_ready, SLOTS)
            turn_rows(pe, xn3, ln_step, LN_STEPS * 3 - NT, x3_turned, x3T_ready, (bank4, bank5), idf)

            def turn_q(u, a, first):
                pe.wait_ge(q3_ready, at(u))
                if not first:
                    pe.wait_ge(qT_ready, 2 * u)
                for g, bank in enumerate((bank4, bank5)):
                    view = bank[:].bitcast(BF16)
                    for h in range(8):
                        ins = pe.transpose(view[0:K3, h * P:(h + 1) * P],
                                           q3row[a][:, 8 * g + h].rearrange("p c d -> p (c d)"), idb)
                    ins.then_inc(q3_turned, 1)

            pe.wait_ge(x3T_ready, NT)
            pe.wait_ge(wq_loaded, 32)

            def project_q(u):
                if u >= 2:
                    pe.wait_ge(qf_done, at(u - 2))
                for c in range(KC):
                    ins = pe.matmul((bank6, bank7)[u % 2][:, :], XT3[:, c, u * P:(u + 1) * P], wq_sb[:, c, :], start=c == 0, stop=c == KC - 1)
                ins.then_inc(q_proj, 1)

            project_q(0)
            for u in range(NT):
                if u + 1 < NT:
                    project_q(u + 1)
                turn_q(u, u % 2, u == 0)

            def a1_scores(h, a, t, first):
                for half in range(2):
                    if not first:
                        pe.wait_ge(s_read, 2 * (8 * h + t) + half - 1)
                    for j in range(2):
                        s = half * 1024 + j * 512
                        ins = pe.matmul(scores[:, s:s + 512], qhead[a][0:K3, t * P:(t + 1) * P], khead[a][0:K3, s:s + 512], start=True, stop=True)
                    ins.then_inc(s_done, 1)

            def a1_turn(h, a, t, first):
                i = t % 2
                pe.wait_ge(p_ready, 8 * h + t + 1)
                for g, (bank, copied) in enumerate(((bank4, pT_lo), (bank5, pT_hi))):
                    if not first:
                        pe.wait_ge(copied, 8 * h + t)
                    else:
                        pe.wait_ge(qT_ready, 2 * NT)
                    view = bank[:].bitcast(BF16)
                    for c in range(8):
                        ins = pe.transpose(view[:, c * P:(c + 1) * P], p16[i][:, (8 * g + c) * P:(8 * g + c + 1) * P].bitcast(BF16), idb)
                    ins.then_inc(p_turned, 1)

            def a1_pv(h, a, t, first):
                i = t % 2
                bank = (bank6, bank7)[a]
                pe.wait_ge(pT_lo, 8 * h + t + 1)
                pe.wait_ge(pT_hi, 8 * h + t + 1)
                if t == 0:
                    pe.wait_ge(v_staged, at(h))
                    if past(h, 2):
                        pe.wait_ge(a_post, 3 * (h - 1))
                for c in range(NC):
                    ins = pe.matmul(bank[:, t * HD:(t + 1) * HD], pT[i][:, c], vhead[a][:, c], start=c == 0, stop=c == NC - 1)
                ins.then_inc(av_done, 1)

            def a1_head(h, a, k, first, last):
                for t in range(NT):
                    if t < NT - 2:
                        a1_scores(h, a, t + 2, False)
                    elif not last:
                        if t == NT - 2:
                            pe.wait_ge(k_loaded[1 - a], 32 * (k + a + 1))
                        a1_scores(h + 1, 1 - a, t + 2 - NT, False)
                    a1_turn(h, a, t, first and t == 0)
                    if t > 0:
                        a1_pv(h, a, t - 1, first)
                    elif not first:
                        a1_pv(h - 1, 1 - a, NT - 1, False)
                if last:
                    a1_pv(h, a, NT - 1, False)

            pe.wait_ge(qf_done, NT)
            pe.wait_ge(h_done, 2 * SLOTS)
            pe.wait_ge(k_loaded[0], 32)
            a1_scores(0, 0, 0, True)
            a1_scores(0, 0, 1, False)
            sweep(pe, H, a1_head)

            for t in range(NT):
                pe.wait_ge(a_post, 3 * H)
                if t >= 2:
                    pe.wait_ge(oT_ready, t - 1)
                else:
                    pe.wait_ge(pT_lo, 8 * H)
                    pe.wait_ge(pT_hi, 8 * H)
                bank = (bank4, bank5)[t % 2]
                for c in range(KC):
                    ins = pe.transpose(bank[:, c * P:(c + 1) * P], oh[:, t, c * P:(c + 1) * P], idf)
                ins.then_inc(o_turned, 1)
            pe.wait_ge(wp_loaded, 32)
            for t in range(NT):
                pe.wait_ge(oT_ready, at(t))
                bank = (bank6, bank7)[t % 2]
                if t >= 2:
                    pe.wait_ge(o_added, 2 * (t - 2) + 1)
                for c in range(KC):
                    ins = pe.matmul(bank[:, :], XT3[:, c, t * P:(t + 1) * P], wp_sb[:, c, :], start=c == 0, stop=c == KC - 1)
                ins.then_inc(o_proj, 1)

            pe.wait_ge(frow_loaded, 32)
            for g in range(FW_GROUPS):
                w, o = g // 8, g % 8
                if g == 16:
                    pe.wait_ge(fd_loaded, 16)
                if g >= 2:
                    pe.wait_ge(fwT_ready, g - 1)
                else:
                    pe.wait_ge(oT_ready, NT)
                view = (bank4, bank5)[g % 2][:].bitcast(BF16)
                for c in range(8):
                    ins = pe.transpose(view[:, c * P:(c + 1) * P], frow[w][:, 2 * o + c // 4, (c % 4) * P:(c % 4 + 1) * P], idb)
                ins.then_inc(fw_turned, 1)
            def turn_x4(t):
                pe.wait_ge(f_step, F_SCALES + xq_step(t))
                bank = (bank6, bank7)[t % 2]
                if t >= 2:
                    pe.wait_ge(x4T_ready, t - 1)
                else:
                    pe.wait_ge(o_added, 2 * NT)
                view = bank[:].bitcast(BF16)
                for c in range(KC):
                    ins = pe.transpose(view[:, c * P:(c + 1) * P], xq4[:, t, c * P:(c + 1) * P], idb)
                ins.then_inc(x4_turned, 1)

            turn_x4(0)
            turn_x4(1)
            pe.wait_ge(fwT_ready, FW_GROUPS)
            for t in range(NT):
                pe.wait_ge(x4T_ready, at(t))
                for q in range(4):
                    n = 4 * t + q
                    for w, bank in ((0, scores[:, (q % 4) * 512:(q % 4) * 512 + 512]), (1, (bank4, bank5)[q % 2][:, :])):
                        if w == 0 and t > 0:
                            pe.wait_ge(fsilu_done, n - 3)
                        if w == 1 and n >= 2:
                            pe.wait_ge(fh_done, n - 1)
                        for c in range(KC):
                            ins = pe.matmul(bank, xT4[:, c, t * P:(t + 1) * P], wT[w][:, c, q * 512:(q + 1) * 512], start=c == 0, stop=c == KC - 1)
                        ins.then_inc(gu_done, 1)
                if t + 2 < NT:
                    turn_x4(t + 2)
            def turn_hidden(t):
                pe.wait_ge(f2_step, 2 * t + 2)
                for g, bank in enumerate((bank4, bank5)):
                    if t:
                        pe.wait_ge(fhT_ready, 2 * (t - 1) + g + 1)
                    view = bank[:].bitcast(BF16)
                    for c in range(8):
                        ins = pe.transpose(view[:, c * P:(c + 1) * P], hqr[t % 2][:, (8 * g + c) * P:(8 * g + c + 1) * P], idb)
                    ins.then_inc(fh_turned, 1)

            turn_hidden(0)
            for t in range(NT):
                if t + 1 < NT:
                    turn_hidden(t + 1)
                pe.wait_ge(fhT_ready, 2 * t + 2)
                bank = (bank6, bank7)[t % 2]
                if t >= 2:
                    pe.wait_ge(fout_done, t - 1)
                for c in range(FC):
                    ins = pe.matmul(bank[:, :], hqT[t % 2][:, c], wdT[:, c], start=c == 0, stop=c == FC - 1)
                ins.then_inc(fdown_done, 1)

        @block.scalar
        def _(act):
            act.dma_start(wkv, Wkv.rearrange("(k p) n -> p k n", p=P)).then_inc(wkv_loaded, 16)
            act.dma_start(bkv_row, bkv.partition_broadcast(P)).then_inc(wkv_loaded, 16)

            def copy_ctx(u, a):
                if past(u, 2):
                    act.wait_ge(v_proj, at(u - 2))
                act.wait_ge(ctx_turned, at(u))
                act.activation(cT[a].rearrange("p c n -> p (c n)"), bank6[:, :], ACT.Copy).then_inc(ctxT_ready, 1)

            def first_part(u, a):
                act.wait_ge(kd_done, at(u))
                act.activation(krow[a][:, :, 0], kd, ACT.Copy).then_inc(kq_done, 1)

            def second_part(u, a):
                act.wait_ge(kqr_done, at(u))
                act.activation(krow[a][:, :, 1], kqr, ACT.Copy).then_inc(kq_done, 1)

            def kv_tile(u, a, k, first, last):
                if first:
                    copy_ctx(0, 0)
                if not last:
                    copy_ctx(u + 1, 1 - a)
                if not first:
                    first_part(u - 1, 1 - a)
                act.wait_ge(ctx_loaded[a], 16 * (k + 1))
                if first:
                    act.wait_ge(ones_set, 1)
                parts = context_parts(u)
                act.activation(parts[:, :, 0:3:2], cin[a].rearrange("p (h o d) -> p h o d", h=H, o=1).broadcast_to([P, H, 2, HD]),
                               ACT.Copy).then_inc(c1_done, 1)
                if not first:
                    second_part(u - 1, 1 - a)
                act.wait_ge(cr_done, at(u))
                act.activation(parts[:, :, 1], by_head(cr), ACT.Copy).then_inc(c2_done, 1)
                if not first:
                    copy_kT(u - 1, 1 - a, k - 1 + a)
                if last:
                    first_part(u, a)
                    second_part(u, a)
                    copy_kT(u, a, k)

            def copy_kT(u, a, k):
                if past(u, 2):
                    act.wait_ge(kst_stored[a], 16 * k)
                for g, bank in enumerate((bank4, bank5)):
                    act.wait_ge(k_turned, 2 * u + g + 1)
                    act.activation(kTbuf[a][0:K3, 8 * g:8 * g + 8].rearrange("p h n -> p (h n)"),
                                   bank[:].bitcast(BF16)[0:K3, :], ACT.Copy).then_inc(kT_ready, 1)

            act.preload_act_table(ACT.Copy)
            sweep(act, NC, kv_tile)

            def std(n):
                act.wait_ge(ln_var, n)
                act.activation(std0, ln_t[:, 0], ACT.Sqrt).then_inc(ln_std, 1)

            std(1)
            act.wait_ge(vmax_ready, 1)
            for b in range(B):
                act.wait_ge(ln_step, LN_STEPS - NT + (b + 1) * QT)
                rows = xn0[:, b * QT:(b + 1) * QT].rearrange("p t (h d) -> p t h d", h=H)
                parts = qrow[:, b].rearrange("p h t (c d) -> p t h c d", d=HD)
                for blk in (2, 3):
                    act.activation(parts[:, :, :, blk], rows, ACT.Copy).then_inc(qs12, 1)
                act.wait_ge(qs_r, b + 1)
                act.activation(parts[:, :, :, 1], qr[:, b * QT:(b + 1) * QT].rearrange("p t (h d) -> p t h d", h=H), ACT.Copy).then_inc(qs12, 1)

            def copy_keys(u, b):
                act.wait_ge(k0_turned, at(u))
                act.activation(kA[b], bank6[:].bitcast(BF16), ACT.Copy).then_inc(ka_ready, 1)

            def copy_m(u, b):
                act.wait_ge(m_turned, at(u))
                act.activation(qC[b][K2:K2 + 2, :], scores[:, 0:512].bitcast(BF16)[K2:K2 + 2, 0:SQ], ACT.Copy).then_inc(m_ready, 1)

            def att_unit(u, a, k, first, last):
                b = 1 - a
                for g in range(4):
                    for j in (2 * g, 2 * g + 1):
                        if j == 2 * g and not first:
                            act.wait_ge(p2_done, 4 * (u - 1) + g + 1)
                        act.wait_ge(st_done, KT * u + j + 1)
                        act.activation(eP[:, OFF[j]:OFF[j] + WID[j]], (bank4, bank5)[j % 2][:, 0:WID[j]], ACT.Exp, scale=SCALE).then_inc(exp_done, 1)
                    if not first:
                        act.wait_ge(pv_done, 4 * (u - 1) + g + 1)
                    act.wait_ge(exp_done, KT * u + 2 * g + 2)
                    s, e = OFF[2 * g], OFF[2 * g + 1] + WID[2 * g + 1]
                    act.activation(p1[:, s:e], eP[:, s:e], ACT.Copy).then_inc(p1_done, 1)
                if within(u + 2, UNITS):
                    copy_keys(u + 2, a)
                if not last:
                    copy_m(u + 1, b)

            act.preload_act_table(ACT.Exp)
            copy_keys(0, 0)
            copy_m(0, 0)
            copy_keys(1, 1)
            sweep(act, UNITS, att_unit)

            def copy_rows(dst, turned, ready, banks):
                for t in range(NT):
                    act.wait_ge(turned, at(t))
                    act.activation(dst[:, :, t * P:(t + 1) * P], banks[t % 2][:].rearrange("p (c n) -> p c n", c=KC), ACT.Copy).then_inc(ready, 1)

            std(2)
            copy_rows(XT, xn_turned, xT_ready, (bank4, bank5))
            act.wait_ge(r_step, 2)
            act.activation(r8[1], r8[0], ACT.Exp).then_inc(r_exp, 1)

            def slot(u, a, k, first, last):
                for half in range(2):
                    if not first:
                        act.wait_ge(h_done, 2 * (u - 1) + half + 1)
                    act.wait_ge(up_done, 4 * u + 2 * half + 1)
                    act.activation(sg[:, half * 512:half * 512 + 512], scores[:, half * 512:half * 512 + 512], ACT.Silu).then_inc(silu_done, 1)
                act.wait_ge(h_turned, 2 * u + 1)
                act.activation(hT[:, 0:4].rearrange("p c n -> p (c n)"), bank4[:, :], ACT.Copy).then_inc(hT0_ready, 1)
                if past(u, 2):
                    act.wait_ge(y_stored[a], 16 * k)
                act.wait_ge(y_done, at(u))
                act.activation(yb[a], bank7[:, :], ACT.Copy).then_inc(y_ready, 1)
                act.wait_ge(y_ready, at(u))
                act.dma_start(ys_d[bass.ds(u * P, P), :], yb[a]).then_inc(y_stored[a], 16)

            act.preload_act_table(ACT.Silu)
            sweep(act, SLOTS, slot)

            std(3)
            copy_rows(XT3, x3_turned, x3T_ready, (bank4, bank5))
            for u in range(NT):
                if u >= 2:
                    act.wait_ge(qst_stored[u % 2], 16 * (u // 2))
                for g, bank in enumerate((bank4, bank5)):
                    act.wait_ge(q3_turned, 2 * u + g + 1)
                    act.activation(qTbuf[u % 2][0:K3, 8 * g:8 * g + 8].rearrange("p h n -> p (h n)"),
                                   bank[:].bitcast(BF16)[0:K3, :], ACT.Copy).then_inc(qT_ready, 1)

            def exp_tile(h, a, t, first):
                i, n = t % 2, 8 * h + t
                if not (first and t < 2):
                    act.wait_ge(p_turned, 2 * n - 2)
                if t == 0 and past(h, 2):
                    act.wait_ge(a_post, 3 * (h - 1))
                act.wait_ge(bias_ready, n + 1)
                act.activation(p16[i], ssb[i], ACT.Exp, bias=ebias[i], scale=-1.0, accum_out=rsum[a][:, t:t + 1]).then_inc(p_ready, 1)

            def a1_head(h, a, k, first, last):
                for t in range(NT):
                    if t < NT - 1:
                        exp_tile(h, a, t + 1, first)
                    elif not last:
                        exp_tile(h + 1, 1 - a, 0, False)
                    act.wait_ge(p_turned, 2 * (8 * h + t) + 2)
                    act.activation(pT[t % 2][:, 8:16].rearrange("p c n -> p (c n)"), bank5[:].bitcast(I16), ACT.Copy).then_inc(pT_hi, 1)

            act.preload_act_table(ACT.Exp)
            exp_tile(0, 0, 0, True)
            sweep(act, H, a1_head)

            copy_rows(XT3, o_turned, oT_ready, (bank4, bank5))

            for g in range(FW_GROUPS):
                if g == 4:
                    std(4)
                w, o = g // 8, g % 8
                act.wait_ge(fw_turned, at(g))
                bank = (bank4, bank5)[g % 2][:].bitcast(BF16)
                if w < 2:
                    dst = wT[w][:, :, 2 * o * P:2 * (o + 1) * P].rearrange("p c (o n) -> p o c n", o=2)
                    act.activation(dst, bank.rearrange("p (o c n) -> p o c n", o=2, c=KC), ACT.Copy).then_inc(fwT_ready, 1)
                else:
                    dst = wdT[:, 8 * (o % 2):8 * (o % 2) + 8, (o // 2) * P:(o // 2 + 1) * P]
                    act.activation(dst, bank.rearrange("p (c n) -> p c n", c=8), ACT.Copy).then_inc(fwT_ready, 1)
            def copy_x4(t):
                act.wait_ge(x4_turned, at(t))
                act.activation(xT4[:, :, t * P:(t + 1) * P], (bank6, bank7)[t % 2][:].bitcast(BF16)[:, 0:KC * P].rearrange("p (c n) -> p c n", c=KC),
                               ACT.Copy).then_inc(x4T_ready, 1)

            copy_x4(0)
            copy_x4(1)
            for t in range(NT):
                for q in range(4):
                    n = 4 * t + q
                    act.wait_ge(gu_done, 2 * n + 1)
                    if n >= 4:
                        act.wait_ge(fh_done, n - 3)
                    act.activation(sgb[:, q * 512:(q + 1) * 512], scores[:, q * 512:(q + 1) * 512], ACT.Silu, scale=gscale[:, 0, t:t + 1]).then_inc(fsilu_done, 1)
                act.wait_ge(fh_done, 4 * t + 4)
                if t:
                    act.wait_ge(fsq_done, t)
                act.activation(hqr[0], hball[:, t], ACT.Square, accum_out=ssq[:, t:t + 1]).then_inc(fsq_done, 1)
                if t + 2 < NT:
                    copy_x4(t + 2)
            act.wait_ge(ln_var, 5)
            act.activation(std0, fsm[:, 0], ACT.Sqrt).then_inc(ln_std, 1)
            for t in range(NT):
                if t >= 2:
                    act.wait_ge(fdown_done, t - 1)
                for g, bank in enumerate((bank4, bank5)):
                    act.wait_ge(fh_turned, 2 * t + g + 1)
                    act.activation(hqT[t % 2][:, 8 * g:8 * g + 8].rearrange("p c n -> p (c n)"), bank[:].bitcast(BF16), ACT.Copy).then_inc(fhT_ready, 1)

        @block.vector
        def _(dve):
            def less_first_part(u, a):
                dve.wait_ge(kq_done, 2 * u + 1)
                dve.wait_ge(kd_done, at(u))
                dve.tensor_tensor(kqr, kd, krow[a][:, :, 0], ALU.subtract).then_inc(kqr_done, 1)

            def third_part(u, a):
                dve.wait_ge(kq_done, 2 * u + 2)
                dve.wait_ge(kqr_done, at(u))
                dve.tensor_tensor(krow[a][:, :, 2], kqr, krow[a][:, :, 1], ALU.subtract).then_inc(krow_ready, 1)

            def kv_tile(u, a, k, first, last):
                parts = context_parts(u)
                if not first:
                    less_first_part(u - 1, 1 - a)
                dve.wait_ge(c1_done, at(u))
                if not first:
                    dve.wait_ge(c3_done, at(u - 1))
                dve.tensor_tensor(by_head(cr), by_head(cin[a]), parts[:, :, 0], ALU.subtract).then_inc(cr_done, 1)
                dve.wait_ge(k_proj, at(u))
                if first:
                    dve.wait_ge(wkv_loaded, 32)
                dve.tensor_tensor(kf.rearrange("p h d -> p (h d)"), scores[:, 0:D], bkv_row[:, 0:D], ALU.add).then_inc(kf_done, 1)
                if not first:
                    third_part(u - 1, 1 - a)
                dve.wait_ge(kf_done, at(u))
                dve.tensor_reduce(kam, kf, X, ALU.max, apply_absolute_value=True).then_inc(k_step, 1)
                dve.wait_ge(k_step, 5 * u + 1)
                dve.tensor_scalar(ks, kam, 1.0 / 127.0, 1e-8, ALU.mult, ALU.max).then_inc(k_step, 1)
                dve.wait_ge(k_step, 5 * u + 2)
                dve.reciprocal(kinv, ks).then_inc(k_step, 1)
                dve.wait_ge(k_step, 5 * u + 3)
                dve.tensor_tensor(kx, kf, each(kinv, [H, HD]), ALU.mult).then_inc(k_step, 1)
                dve.wait_ge(k_step, 5 * u + 4)
                dve.tensor_scalar(kr, kx, MAGIC, MAGIC, ALU.add, ALU.subtract).then_inc(k_step, 1)
                dve.wait_ge(k_step, 5 * u + 5)
                dve.tensor_tensor(kd, kr, each(ks, [H, HD]), ALU.mult).then_inc(kd_done, 1)
                dve.wait_ge(v_proj, at(u))
                dve.tensor_tensor(vf[:, bass.ds(u, 1)].rearrange("p u d -> p (u d)"), scores[:, D:2 * D], bkv_row[:, D:2 * D], ALU.add).then_inc(vf_done, 1)
                dve.wait_ge(c2_done, at(u))
                dve.tensor_tensor(parts[:, :, 3], by_head(cr), parts[:, :, 1], ALU.subtract).then_inc(c3_done, 1)
                dve.wait_ge(wpiece_loaded[a], 48 * (k + 1))
                dve.tensor_reduce(wsums[:, bass.ds(u, 1)].rearrange("p u w -> p (u w)"), wpiece[a], X, ALU.add,
                                  apply_absolute_value=True).then_inc(wpiece_done, 1)
                if last:
                    less_first_part(u, a)
                    third_part(u, a)

            sweep(dve, NC, kv_tile)
            dve.wait_ge(wpiece_done, NC)
            dve.tensor_reduce(wst[:, 0], wsums.rearrange("p u w -> p w u"), X, ALU.add).then_inc(wsum_done, 1)
            dve.wait_ge(vf_done, NC)
            dve.tensor_reduce(vam, vf.rearrange("p t d -> p d t"), X, ALU.max, apply_absolute_value=True).then_inc(v_step, 1)

            dve.wait_ge(wsum_all, 1)
            dve.tensor_scalar(wst[:, 2], wst[:, 1], 1.0 / (FI * D), 1e-5, ALU.mult, ALU.max).then_inc(w_mean, 1)
            dve.wait_ge(w_mean, 1)
            for j, half in ((3, 0.5), (4, -0.5)):
                dve.tensor_scalar(wst[:, j], wst[:, 2], half, None, ALU.mult).then_inc(w_mean, 1)

            def rsqrt(var, std, tmp, ready, step, n):
                dve.wait_ge(ready[0], ready[1])
                for ins in (lambda: dve.reciprocal(tmp[:, 1], std),
                            lambda: dve.tensor_tensor(tmp[:, 2], var, tmp[:, 1], ALU.mult),
                            lambda: dve.tensor_tensor(tmp[:, 3], tmp[:, 2], std, ALU.add),
                            lambda: dve.reciprocal(tmp[:, 4], tmp[:, 3]),
                            lambda: dve.tensor_scalar(tmp[:, 1], tmp[:, 4], 2.0, None, ALU.mult)):
                    ins().then_inc(step, 1)
                    n += 1
                    dve.wait_ge(step, n)
                return n

            def tile_stats(j, t):
                dve.bn_stats(stats[:, t], xres[:, t]).then_inc(ln_step, 1)
                dve.wait_ge(ln_step, LN_STEPS * j + 2 * t + 1)
                dve.bn_aggr(mv[:, t], stats[:, t]).then_inc(ln_step, 1)

            def layer_norm(j, dst):
                n = LN_STEPS * j + 2 * NT
                dve.wait_ge(ln_step, n)
                dve.tensor_scalar(ln_t[:, 0], mv[:, :, 1], LN_EPS, None, ALU.add).then_inc(ln_var, 1)
                dve.wait_ge(ln_var, j + 1)
                n = rsqrt(ln_t[:, 0], std0, ln_t, (ln_std, j + 1), ln_step, n)
                dve.scalar_tensor_tensor(ln_t[:, 5], mv[:, :, 0], -1.0, ln_t[:, 1], ALU.mult, ALU.mult).then_inc(ln_step, 1)
                n += 1
                dve.wait_ge(ln_step, n)
                for t in range(NT):
                    dve.tensor_scalar(dst[:, t], xres[:, t], ln_t[:, 1, t:t + 1], ln_t[:, 5, t:t + 1], ALU.mult, ALU.add).then_inc(ln_step, 1)
                assert n + NT == LN_STEPS * (j + 1)

            for b in range(B):
                dve.wait_ge(x_loaded[b], 16)
            for a in range(2):
                dve.wait_ge(kst_stored[a], 16 * (NC // 2))
            dve.wait_ge(v_step, 1)
            dve.wait_ge(v_stored, 16 * NC)
            dve.wait_ge(krow_ready, NC)
            for t in range(NT):
                tile_stats(0, t)
            layer_norm(0, xn0)
            for b in range(B):
                s = slice(b * QT, (b + 1) * QT)
                rows = xn0[:, s].rearrange("p t (h d) -> p t h d", h=H)
                rest = qr[:, s].rearrange("p t (h d) -> p t h d", h=H)
                parts = qrow[:, b].rearrange("p h t (c d) -> p t h c d", d=HD)
                dve.wait_ge(qs12, 3 * b + 1)
                dve.wait_ge(ln_step, LN_STEPS)
                dve.tensor_tensor(rest, rows, parts[:, :, :, 2], ALU.subtract).then_inc(qs_r, 1)
                dve.tensor_copy(parts[:, :, :, 4], rows).then_inc(qs3, 1)
                dve.wait_ge(qs12, 3 * b + 3)
                dve.wait_ge(qs_r, b + 1)
                dve.tensor_tensor(parts[:, :, :, 0], rest, parts[:, :, :, 1], ALU.subtract).then_inc(qs3, 1)
            dve.wait_ge(qs3, 2 * B)
            dve.wait_ge(qs12, 3 * B)
            dve.wait_ge(c3_done, NC)
            dve.wait_ge(c2_done, NC)
            dve.wait_ge(xs_zeroed, 16 * SLOTS)
            dve.memset(rl, 1.0).then_inc(qrow_ready, 1)

            def copy_keys(u, b):
                dve.wait_ge(ka_ready, at(u))
                dve.tensor_copy(kC[b][0:K2], kA[b][0:K2]).then_inc(kc_ready, 1)

            def copy_q(u, b):
                dve.wait_ge(q_turned, at(u))
                dve.tensor_copy(qA[b], bank6[:].bitcast(BF16)[:, 0:SQ]).then_inc(q_ready, 1)
                dve.tensor_copy(qC[b][0:K2], bank6[:].bitcast(BF16)[0:K2, SQ:2 * SQ]).then_inc(q_ready, 1)

            def take_max(u, t):
                s = 1024 * (t % 2)
                dve.wait_ge(smax_done, QT * u + t + 1)
                dve.reduce_max(mx[:, t:t + 1], scores[:, s:s + 512 + (t + 1) * P], X).then_inc(max_done, 1)

            def split_m(u, first):
                dve.wait_ge(max_done, QT * u + QT)
                if not first:
                    dve.wait_ge(m_turned, at(u - 1))
                dve.tensor_scalar(mparts[:, :, 0], mx, -1.0, None, ALU.mult).then_inc(m_step, 1)
                dve.wait_ge(m_step, 2 * u + 1)
                dve.scalar_tensor_tensor(mparts[:, :, 1], mx, -1.0, mparts[:, :, 0], ALU.mult, ALU.subtract).then_inc(m_step, 1)

            def rest_of_p(u, g):
                s, e = OFF[2 * g], OFF[2 * g + 1] + WID[2 * g + 1]
                dve.wait_ge(p1_done, 4 * u + g + 1)
                dve.tensor_tensor(p2[:, s:e], eP[:, s:e], p1[:, s:e], ALU.subtract).then_inc(p2_done, 1)

            def finish_unit(u, first):
                dve.wait_ge(pv_done, 4 * u + 4)
                if not first:
                    dve.wait_ge(o_done, at(u - 1))
                dve.tensor_reduce(osum, bank7[:, 0:4 * 97].rearrange("p (t c) -> p t c", t=QT)[:, :, 0:K3].rearrange("p t (c d) -> p t d c", d=HD),
                                  X, ALU.add).then_inc(oread_done, 1)
                dve.reciprocal(rl, bank7[:, 96:4 * 97:97]).then_inc(oread_done, 1)
                dve.wait_ge(oread_done, 2 * u + 2)
                dve.tensor_tensor(oatt.rearrange("p b h t d -> p (b h) t d")[:, bass.ds(u, 1)].rearrange("p u t d -> p (u t) d"),
                                  osum, each(rl, [QT, HD]), ALU.mult).then_inc(o_done, 1)

            def att_unit(u, a, k, first, last):
                b = 1 - a
                if not first:
                    finish_unit(u - 1, not past(u, 2))
                if not last:
                    take_max(u + 1, 0)
                    take_max(u + 1, 1)
                rest_of_p(u, 0)
                if not last:
                    take_max(u + 1, 2)
                rest_of_p(u, 1)
                if not last:
                    take_max(u + 1, 3)
                    split_m(u + 1, False)
                rest_of_p(u, 2)
                if within(u + 2, UNITS):
                    copy_keys(u + 2, a)
                rest_of_p(u, 3)
                if within(u + 2, UNITS):
                    copy_q(u + 2, a)
                if last:
                    finish_unit(u, False)

            copy_keys(0, 0)
            copy_q(0, 0)
            for t in range(QT):
                take_max(0, t)
            split_m(0, True)
            copy_keys(1, 1)
            copy_q(1, 1)
            sweep(dve, UNITS, att_unit)
            dve.wait_ge(o_done, UNITS)
            for t in range(NT):
                dve.tensor_tensor(by_head(xres[:, t]), by_head(xres[:, t]), oatt[:, t // QT, :, t % QT], ALU.add).then_inc(att_added, 1)
                dve.wait_ge(att_added, at(t))
                tile_stats(1, t)

            layer_norm(1, xn)
            dve.wait_ge(gw_turned, 1)
            dve.tensor_copy(gwT.rearrange("p c e -> p (c e)"), bank6[:, 0:KC * E]).then_inc(gwT_ready, 1)
            n = 0

            def r(ins):
                nonlocal n
                ins.then_inc(r_step, 1)
                n += 1
                dve.wait_ge(r_step, n)

            te8 = [NT, E]
            ramp = iota_e.rearrange("p (o e) -> p o e", o=1).broadcast_to([P] + te8)
            logits = bank7[:, 0:NT * E].rearrange("p (t e) -> p t e", t=NT)
            dve.wait_ge(logits_done, 1)
            r(dve.tensor_reduce(r1[0], logits, X, ALU.max))
            r(dve.tensor_tensor(r8[0], logits, each(r1[0], te8), ALU.subtract))
            dve.wait_ge(r_exp, 1)
            r(dve.tensor_reduce(r1[1], r8[1], X, ALU.add))
            r(dve.reciprocal(r1[2], r1[1]))
            r(dve.tensor_tensor(r8[2], r8[1], each(r1[2], te8), ALU.mult))
            for left, best, cand, hot in ((2, 3, 4, 5), (6, 5, 4, 7)):
                r(dve.tensor_reduce(r1[best], r8[left], X, ALU.max))
                r(dve.tensor_tensor(r8[3], r8[left], each(r1[best], te8), ALU.is_equal))
                r(dve.scalar_tensor_tensor(r8[cand], r8[3], -100.0, ramp, ALU.mult, ALU.add))
                r(dve.tensor_reduce(r1[4], r8[cand], X, ALU.min))
                r(dve.tensor_tensor(r8[hot], r8[cand], each(r1[4], te8), ALU.is_equal))
                if hot == 5:
                    r(dve.scalar_tensor_tensor(r8[6], r8[5], -2.0, r8[2], ALU.mult, ALU.add))
            r(dve.tensor_tensor(asg, r8[5], r8[7], ALU.add))
            assert n == R_ASSIGNED
            r(dve.tensor_tensor(r1[6], r1[3], r1[5], ALU.add))
            r(dve.reciprocal(r1[7], r1[6]))
            r(dve.tensor_tensor(r1[8], r1[3], r1[7], ALU.mult))
            r(dve.tensor_tensor(r1[9], r1[5], r1[7], ALU.mult))
            dve.wait_ge(ranks_done, 1)
            r(dve.tensor_scalar(te[0], bank7[:, 128:128 + E], 1.0 / P, 127.0 / 128.0 - 0.5 + 1.0 / 256.0, ALU.mult, ALU.add))
            r(dve.tensor_scalar(te[1], te[0], MAGIC, MAGIC, ALU.add, ALU.subtract))
            r(dve.tensor_tensor_scan(te[2], ones[:, 0:E], te[1], 0.0, ALU.mult, ALU.add))
            r(dve.tensor_tensor(te[3], te[2], te[1], ALU.subtract))
            r(dve.tensor_scalar(te[4], te[3], float(P), None, ALU.mult))
            r(dve.tensor_tensor(r8[8], bank6[:, 0:NT * E].rearrange("p (t e) -> p t e", t=NT),
                                te[4].rearrange("p (o e) -> p o e", o=1).broadcast_to([P] + te8), ALU.add))
            for j, hot in ((0, 5), (1, 7)):
                r(dve.tensor_tensor(r8[9 + j], r8[hot], r8[8], ALU.mult))
                r(dve.tensor_reduce(r1[j], r8[9 + j], X, ALU.add))
            for j in range(2):
                r(dve.tensor_copy(posi[:, j], r1[j]))
            r(dve.tensor_tensor(cmp, te[2].rearrange("p (o e) -> p o e", o=1).broadcast_to([P, SLOTS + 1, E]),
                                each(iota_s, [SLOTS + 1, E]), ALU.is_le))
            r(dve.tensor_reduce(slot_f, cmp, X, ALU.add))
            r(dve.tensor_scalar(slot_e, slot_f, float(E - 1), None, ALU.min))
            assert n == R_STEPS
            dve.wait_ge(vmax_ready, 1)
            dve.tensor_scalar(svrow, svrow, 1.0 / 127.0, 1e-8, ALU.mult, ALU.max).then_inc(v_step, 1)
            dve.wait_ge(v_step, 2)
            dve.reciprocal(vinv, svrow).then_inc(v_step, 1)

            def copy_slot(u, a):
                dve.wait_ge(xs_turned, at(u))
                dve.tensor_copy(xsT[a].rearrange("p c n -> p (c n)"), bank6[:, :]).then_inc(xsT_ready, 1)

            def slot(u, a, k, first, last):
                for half in range(2):
                    if not first:
                        dve.wait_ge(h_turned, 2 * (u - 1) + half + 1)
                    dve.wait_ge(silu_done, 2 * u + half + 1)
                    dve.wait_ge(up_done, 4 * u + 2 * half + 2)
                    dve.tensor_tensor(hb[:, half * 512:half * 512 + 512], scores[:, 1024 + half * 512:1536 + half * 512],
                                      sg[:, half * 512:half * 512 + 512], ALU.mult).then_inc(h_done, 1)
                if not last:
                    copy_slot(u + 1, 1 - a)
                dve.wait_ge(h_turned, 2 * u + 2)
                dve.tensor_copy(hT[:, 4:8].rearrange("p c n -> p (c n)"), bank5[:, :]).then_inc(hT1_ready, 1)

            copy_slot(0, 0)
            sweep(dve, SLOTS, slot)
            for t in range(NT):
                dve.wait_ge(gathered[t // 2], 64)
                for j in range(2):
                    if j:
                        dve.wait_ge(moe_added, 2 * t + 1)
                    dve.scalar_tensor_tensor(xres[:, t], grow[2 * t + j], r1[8 + j][:, t:t + 1], xres[:, t], ALU.mult, ALU.add).then_inc(moe_added, 1)
                dve.wait_ge(moe_added, 2 * t + 2)
                tile_stats(2, t)
            dve.wait_ge(moe_added, 2 * NT)

            layer_norm(2, xn3)
            dve.wait_ge(wq_loaded, 32)
            n = 0

            def q(ins):
                nonlocal n
                ins.then_inc(q_step, 1)
                n += 1
                dve.wait_ge(q_step, n)

            for u in range(NT):
                a = u % 2
                dve.wait_ge(q_proj, at(u))
                dve.tensor_tensor(qf.rearrange("p h d -> p (h d)"), (bank6, bank7)[u % 2][:, :], bq_row, ALU.add).then_inc(qf_done, 1)
                dve.wait_ge(qf_done, at(u))
                q(dve.tensor_reduce(qam, qf, X, ALU.max, apply_absolute_value=True))
                q(dve.tensor_scalar(qsv, qam, SCALE / 127.0, 1e-8, ALU.mult, ALU.max))
                q(dve.tensor_scalar(nsq[:, :, u], qsv, -1.0, None, ALU.mult))
                q(dve.reciprocal(qinv, qsv))
                q(dve.tensor_scalar(qam, qinv, SCALE, None, ALU.mult))
                q(dve.tensor_tensor(qx, qf, each(qam, [H, HD]), ALU.mult))
                if u >= 2:
                    dve.wait_ge(q3_turned, 2 * (u - 1))
                dve.tensor_scalar(q3row[a], qx.rearrange("p h (o d) -> p h o d", o=1).broadcast_to([P, H, 3, HD]), MAGIC, MAGIC,
                                  ALU.add, ALU.subtract).then_inc(q3_ready, 1)

            def read_scores(h, a, t, first):
                i, n = t % 2, 8 * h + t
                if not (first and t < 2):
                    dve.wait_ge(p_ready, n - 1)
                for half in range(2):
                    s = half * 1024
                    dve.wait_ge(s_done, 2 * n + half + 1)
                    dve.tensor_scalar(ssb[i][:, s:s + 1024], scores[:, s:s + 1024], nsq[:, bass.ds(h, 1), t], None, ALU.mult, ALU.min,
                                      accum_out=nmx[i][:, half:half + 1]).then_inc(s_read, 1)

            def make_bias(h, t):
                i, n = t % 2, 8 * h + t
                dve.wait_ge(s_read, 2 * n + 2)
                dve.tensor_scalar(ebias[i], nmx[i][:, 0:1], nmx[i][:, 1:2], LN255, ALU.min, ALU.add).then_inc(bias_ready, 1)

            def finish_head(h, a):
                bank = (bank6, bank7)[a]
                dve.wait_ge(av_done, 8 * (h + 1))
                dve.reciprocal(rrec, rsum[a]).then_inc(a_post, 1)
                dve.wait_ge(a_post, 3 * h + 1)
                dve.tensor_tensor(otmp, bank[:, 0:NT * HD].rearrange("p (t d) -> p t d", t=NT), each(rrec, [NT, HD]), ALU.mult).then_inc(a_post, 1)
                dve.wait_ge(a_post, 3 * h + 2)
                dve.tensor_tensor(oh[:, :, bass.ds(h * HD, HD)], otmp,
                                  svrow[:, bass.ds(h * HD, HD)].rearrange("p (o d) -> p o d", o=1).broadcast_to([P, NT, HD]), ALU.mult).then_inc(a_post, 1)

            def a1_head(h, a, k, first, last):
                for t in range(NT):
                    if t < NT - 2:
                        read_scores(h, a, t + 2, first)
                    elif not last:
                        read_scores(h + 1, 1 - a, t + 2 - NT, False)
                    dve.wait_ge(p_turned, 2 * (8 * h + t) + 1)
                    dve.tensor_copy(pT[t % 2][:, 0:8].rearrange("p c n -> p (c n)"), bank4[:].bitcast(I16)).then_inc(pT_lo, 1)
                    if t < NT - 2:
                        make_bias(h, t + 2)
                    elif not last:
                        make_bias(h + 1, t + 2 - NT)
                    if t == 2 and not first:
                        finish_head(h - 1, 1 - a)
                if last:
                    finish_head(h, a)

            dve.wait_ge(q_step, 6 * NT)
            for t in range(2):
                read_scores(0, 0, t, True)
                make_bias(0, t)
            sweep(dve, H, a1_head)

            dve.wait_ge(wp_loaded, 32)
            for t in range(NT):
                dve.wait_ge(o_proj, at(t))
                dve.tensor_tensor(xres[:, t], (bank6, bank7)[t % 2][:, :], xres[:, t], ALU.add).then_inc(o_added, 1)
                dve.wait_ge(o_added, 2 * t + 1)
                dve.tensor_tensor(xres[:, t], xres[:, t], bp_row, ALU.add).then_inc(o_added, 1)
                dve.wait_ge(o_added, 2 * t + 2)
                tile_stats(3, t)
            dve.wait_ge(o_added, 2 * NT)

            layer_norm(3, xn4)
            dve.wait_ge(ln_step, 4 * LN_STEPS)
            n = 0

            def s(ins):
                nonlocal n
                ins.then_inc(f_step, 1)
                n += 1
                dve.wait_ge(f_step, n)

            s(dve.tensor_reduce(am4, xn4, X, ALU.max, apply_absolute_value=True))
            s(dve.tensor_scalar(sx4, am4, 1e-5, None, ALU.max))
            s(dve.reciprocal(sr4, sx4))
            s(dve.tensor_scalar(am4, sr4, 127.0, None, ALU.mult))
            s(dve.tensor_scalar(sr4, sx4, 1.0 / 127.0, None, ALU.mult))
            for w in range(2):
                s(dve.tensor_scalar(gscale[:, w], sr4, wst[:, 2, w:w + 1], None, ALU.mult))
            assert n == F_SCALES
            for t in range(NT + 1):
                if t < NT:
                    dve.tensor_scalar(xn4[:, t], xn4[:, t], am4[:, t:t + 1], MAGIC, ALU.mult, ALU.add).then_inc(f_step, 1)
                if t:
                    dve.wait_ge(f_step, F_SCALES + max(1, 2 * (t - 1)))
                    dve.tensor_scalar(xq4[:, t - 1], xn4[:, t - 1], MAGIC, None, ALU.subtract).then_inc(f_step, 1)
            n += 2 * NT
            assert n == F_STEPS_Q

            dve.wait_ge(fwT_ready, FW_GROUPS)
            hm = fsm[:, 6]

            def norm_hidden(t):
                dve.wait_ge(fy_done, at(t))
                dve.tensor_reduce(hm[:, t:t + 1], hball[:, t], X, ALU.max, apply_absolute_value=True).then_inc(fmax_done, 1)

            for t in range(NT):
                for q4 in range(4):
                    m = 4 * t + q4
                    dve.wait_ge(gu_done, 2 * m + 2)
                    dve.wait_ge(fsilu_done, at(m))
                    dve.scalar_tensor_tensor(hball[:, t, q4 * 512:(q4 + 1) * 512], (bank4, bank5)[q4 % 2][:, :], gscale[:, 1, t:t + 1],
                                             sgb[:, q4 * 512:(q4 + 1) * 512], ALU.mult, ALU.mult).then_inc(fh_done, 1)
                if t >= 2:
                    norm_hidden(t - 2)
            for t in (NT - 2, NT - 1):
                norm_hidden(t)
            dve.tensor_scalar(fsm[:, 0], ssq, 1.0 / FI, RMS_EPS, ALU.mult, ALU.add).then_inc(ln_var, 1)
            dve.wait_ge(ln_var, 5)
            n = 0
            n = rsqrt(fsm[:, 0], std0, fsm, (ln_std, 5), f_step, F_STEPS_Q)
            dve.wait_ge(fmax_done, NT)
            s(dve.tensor_tensor(fsm[:, 7], fsm[:, 1], hm, ALU.mult))
            s(dve.tensor_scalar(fsm[:, 8], fsm[:, 7], 1e-5, None, ALU.max))
            s(dve.reciprocal(fsm[:, 9], fsm[:, 8]))
            s(dve.scalar_tensor_tensor(fsm[:, 10], fsm[:, 9], 127.0, fsm[:, 1], ALU.mult, ALU.mult))
            s(dve.tensor_scalar(fsm[:, 11], fsm[:, 8], 1.0 / 127.0, wst[:, 2, 2:3], ALU.mult, ALU.mult))

            def add_down(t):
                dve.wait_ge(fdown_done, at(t))
                dve.scalar_tensor_tensor(xres[:, t], (bank6, bank7)[t % 2][:, :], fsm[:, 11, t:t + 1], xres[:, t], ALU.mult, ALU.add).then_inc(fout_done, 1)

            for t in range(NT):
                dve.tensor_scalar(hball[:, t], hball[:, t], fsm[:, 10, t:t + 1], MAGIC, ALU.mult, ALU.add).then_inc(f2_step, 1)
                dve.wait_ge(f2_step, 2 * t + 1)
                if t >= 2:
                    dve.wait_ge(fh_turned, 2 * (t - 1))
                dve.tensor_scalar(hqr[t % 2], hball[:, t], MAGIC, None, ALU.subtract).then_inc(f2_step, 1)
                if t >= 2:
                    add_down(t - 2)
            for t in (NT - 2, NT - 1):
                add_down(t)


_INS = ["x", "ctx_2048", "L0_ffn_gate_w", "L0_ffn_w1", "L0_ffn_w2", "L0_ffn_w3", "L1_xattn_Wq", "L1_xattn_bq", "L1_xattn_Wkv",
        "L1_xattn_bkv", "L1_xattn_Wp", "L1_xattn_bp", "L1_ffn_w_gate", "L1_ffn_w_up", "L1_ffn_w_down", "L1_ffn_ln_weight"]


def kernel(**inputs):
    import numpy as np
    import concourse.bacc as bacc
    from concourse.bass_utils import run_bass_kernel_spmd

    nc = bacc.Bacc("TRN2", target_bir_lowering=False, num_devices=1)
    arrays, args = {}, []
    for name in _INS:
        a = np.ascontiguousarray(inputs[name])
        arrays[f"in_{name}"] = a
        args.append(nc.dram_tensor(f"in_{name}", a.shape, mybir.dt.from_np(a.dtype), kind="ExternalInput").ap())
    args.append(nc.dram_tensor("out_0", (B, SQ, D), F32, kind="ExternalOutput").ap())
    program(nc, *args)
    return run_bass_kernel_spmd(nc, [arrays], core_ids=[0]).results[0]["out_0"]
```
